# Optimizing a Trainium2 kernel written in Bass

```python
import numpy as np
import jax
import jax.numpy as jnp

def _softmax(x, axis=-1):
    return jax.nn.softmax(x, axis=axis)

def _gelu(x):
    return jax.nn.gelu(x, approximate=True)

def _silu(x):
    return jax.nn.silu(x)

def _sigmoid(x):
    return jax.nn.sigmoid(x)

def _layernorm(x, axis=-1, eps=1e-05):
    m = jnp.mean(x, axis=axis, keepdims=True)
    v = jnp.var(x, axis=axis, keepdims=True)
    return (x - m) / jnp.sqrt(v + eps)

def _scatter_add(tgt, idx, src, axis=0):
    return tgt.at[idx].add(src)

def _segment_sum(src, seg, n):
    return jax.ops.segment_sum(src, seg, n)
kernel_name = 'mk_cond_resid_d1_seqx_r4_3d30c1'

def setup_inputs(seed: int=0):
    np.random.seed(seed)
    _w = jnp.asarray

    def _rec_inputs():
        import jax
        import jax.numpy as jnp
        _rk = jax.random.key(seed)
        x = -0.0003929 + 0.9999 * jax.random.normal(jax.random.fold_in(_rk, 1), (64, 64, 256), jnp.float32)
        _lenS = 64 - jax.random.randint(jax.random.fold_in(_rk, 7), (64,), 0, max(1, 64 // 4) + 1, jnp.int32)
        _lenS2 = 64 - jax.random.randint(jax.random.fold_in(_rk, 8), (64,), 0, max(1, 64 // 4) + 1, jnp.int32)
        itok_B_0_2 = jax.random.randint(jax.random.fold_in(_rk, 11), (64,), 0, 3, jnp.int32)
        return (x, itok_B_0_2)
    x, itok_B_0_2 = _rec_inputs()

    def _L0_cond_setup():
        import jax, jax.numpy as jnp
        import numpy as np
        B, S, D, F, E = (8, 512, 256, 1024, 5)

        def _dense(x, wi_, wo_):
            return jax.nn.relu(x @ wi_) @ wo_
        key = jax.random.key(seed)
        ks = jax.random.split(key, 9)
        sc = 0.02
        return {'hidden_states': jax.random.normal(ks[0], (B, S, D), jnp.float32), 'type_label': jax.random.randint(ks[1], (B,), 0, E, jnp.int32), 'wi': jax.random.normal(ks[2], (E, D, F), jnp.float32) * sc, 'wo': jax.random.normal(ks[3], (E, F, D), jnp.float32) * sc, 'swi': jax.random.normal(ks[4], (2, D, F), jnp.float32) * sc, 'swo': jax.random.normal(ks[5], (2, F, D), jnp.float32) * sc, 'g1': jax.random.normal(ks[6], (3 * D, D), jnp.float32) * sc, 'g2': jax.random.normal(ks[7], (D, 3), jnp.float32) * sc}
    _L0_cond_all = _L0_cond_setup()
    _L0_cond_in = {k: v for k, v in _L0_cond_all.items() if k in ('wi', 'wo', 'swi', 'swo', 'g1', 'g2')}
    del _L0_cond_all
    return {'x': x, 'itok_B_0_2': itok_B_0_2, 'L0_cond_wi': _L0_cond_in['wi'], 'L0_cond_wo': _L0_cond_in['wo'], 'L0_cond_swi': _L0_cond_in['swi'], 'L0_cond_swo': _L0_cond_in['swo'], 'L0_cond_g1': _L0_cond_in['g1'], 'L0_cond_g2': _L0_cond_in['g2']}

def reference(x, itok_B_0_2, L0_cond_wi, L0_cond_wo, L0_cond_swi, L0_cond_swo, L0_cond_g1, L0_cond_g2):
    import jax
    import jax.numpy as jnp

    def _L0_cond_ref(hidden_states, type_label, wi, wo, swi, swo, g1, g2):
        import jax, jax.numpy as jnp
        import numpy as np
        B, S, D, F, E = (8, 512, 256, 1024, 5)

        def _dense(x, wi_, wo_):
            return jax.nn.relu(x @ wi_) @ wo_
        x = hidden_states
        s0 = _dense(x, swi[0], swo[0])
        s1 = _dense(x, swi[1], swo[1])
        wi_sel = wi[type_label]
        wo_sel = wo[type_label]
        h = jax.nn.relu(jnp.einsum('bsd,bdf->bsf', x, wi_sel))
        eo = jnp.einsum('bsf,bfd->bsd', h, wo_sel)
        gate_in = jnp.concatenate([eo[:, 0], s0[:, 0], s1[:, 0]], axis=-1)
        w = jax.nn.softmax(jax.nn.relu(gate_in @ g1) @ g2, axis=-1)
        w = w[:, :, None, None]
        return eo * w[:, 0] + s0 * w[:, 1] + s1 * w[:, 2]
    x = x + _L0_cond_ref(x, itok_B_0_2, L0_cond_wi, L0_cond_wo, L0_cond_swi, L0_cond_swo, L0_cond_g1, L0_cond_g2)
    return x

_drawn_inputs = setup_inputs


def setup_inputs(seed=0):
    import zlib

    import numpy as np

    out = dict(_drawn_inputs(seed))
    spreads = {}
    factors = {'L0_cond_g1': 8.0, 'L0_cond_g2': 8.0}
    for name, (base, spread) in spreads.items():
        noise = np.random.default_rng([zlib.crc32(name.encode()), seed]).standard_normal(out[name].shape)
        drawn = base * np.exp(spread * noise) if base else spread * noise
        out[name] = jnp.asarray(drawn.astype(out[name].dtype))
    for name, factor in factors.items():
        out[name] = (out[name] * factor).astype(out[name].dtype)
    return out
```

```python
from contextlib import ExitStack

import concourse.bass as bass
from concourse import mybir

F32 = mybir.dt.float32
F16 = mybir.dt.float16
I32 = mybir.dt.int32
ALU = mybir.AluOpType
ACT = mybir.ActivationFunctionType
AX = mybir.AxisListType
ABSMAX = bass.bass_isa.ReduceOp.absmax

P = 128



def build(nc, x, labels, wi, wo, swi, swo, g1, g2, out):
    B, S, D = x.shape
    NE, _, F = wi.shape
    NSH = swi.shape[0]
    DC = D // P
    FC = F // P
    TG = 4
    TOK = TG * P
    TILES = B * S // TOK
    SLOTS = 4
    EG = SLOTS * S // P
    ETOK = SLOTS * S
    JOBS = (B + NE * (SLOTS - 1)) // SLOTS
    NSLOT = JOBS * SLOTS
    GROUPS = B * S // P
    PERTILE = TOK // S
    K3 = 1 + NSH
    WCOL = DC * F
    assert WCOL == FC * D and S == 64 and JOBS % 2 == 1 and TILES == 8 and B <= P

    LAG, RING, NP1 = 2, 4, 2
    SH = NSH * FC
    STEP_M = SH
    STEP_E = 2 * SH
    STEP_B = STEP_E + FC * JOBS

    def e_step(t):
        return STEP_E + FC * t

    def b_step(u):
        return STEP_B + SH * (u - 1)

    def e_x(t):
        return 1 + t

    def b_x(u):
        return JOBS + u

    def e_drained(t):
        return 5 + t

    NW = 2 * NSH + 2 * NE
    STAGES = 4

    ctx = ExitStack()
    with ctx:
        def sb(name, shape, dt=F32):
            return ctx.enter_context(nc.sbuf_tensor(name, shape, dt))

        def sem(name):
            return ctx.enter_context(nc.semaphore(name))

        scratch = nc.dram_tensor("expert_rows", (B + NSLOT, S, D), F32, kind="Internal").ap()

        w_exp = sb("w_exp", [P, NE, 4 * WCOL], F16)
        w_sh = sb("w_sh", [P, NSH, 4 * WCOL], F16)
        region = sb("region", [P, 4 * WCOL], F32)
        stage = [region[:, s * WCOL:(s + 1) * WCOL] for s in range(STAGES)]
        w_now = [region[:, 2 * s * WCOL:2 * (s + 1) * WCOL].bitcast(F16) for s in range(2)]
        rg = region[:, :].rearrange("p (b g d) -> p b g d", g=TG, d=D)
        e_nat = [rg[:, i] for i in range(2)]
        acc = [rg[:, 2 + i] for i in range(2)]
        x_t0, e_t0 = rg[:, 4], rg[:, 5]
        x_nat = sb("x_nat", [P, 2, TG, D])
        x_hi = sb("x_hi", [P, TG, D], F16)
        x_lo = sb("x_lo", [P, TG, D], F16)
        x_T = sb("x_T", [P, 2, 2, DC, TOK], F16)
        h_hi = sb("h_hi", [P, RING, TOK], F16)
        h_lo = sb("h_lo", [P, RING, TOK], F16)
        e_out = sb("e_out", [P, 2, EG, D])
        s_t0 = sb("s_t0", [P, NSH, TG, D])
        f_nat = sb("f_nat", [B, D])
        f_hi = sb("f_hi", [B, D], F16)
        f_lo = sb("f_lo", [B, D], F16)
        f_T = sb("f_T", [P, 2, DC, B], F16)
        x_max = sb("x_max", [P, TG]); x_pow = sb("x_pow", [P, TG]); x_cl = sb("x_cl", [P, TG])
        x_scale = sb("x_scale", [P, TG])
        x_inv = sb("x_inv", [P, 2, TG]); x_inv0 = sb("x_inv0", [P, TG])
        f_max = sb("f_max", [B, 1]); f_pow = sb("f_pow", [B, 1]); f_cl = sb("f_cl", [B, 1])
        f_scale = sb("f_scale", [B, 1]); f_inv = sb("f_inv", [B, 1])
        w_max = sb("w_max", [P, NW]); w_all = sb("w_all", [P, NW]); w_pow = sb("w_pow", [P, NW])
        w_cl = sb("w_cl", [P, NW])
        w_scale = sb("w_scale", [P, NW])
        w_inv = sb("w_inv", [P, NW // 2, 2])
        pair_inv = sb("pair_inv", [P, NW // 2])
        identf = sb("identf", [P, P]); ident = sb("ident", [P, P], F16)
        ones = sb("ones", [B, B])
        lower = sb("lower", [B, B])
        slot_no = sb("slot_no", [B, NSLOT])
        label_no = sb("label_no", [B, NE])
        job_no = sb("job_no", [1, JOBS, NE - 1])
        batch_no = sb("batch_no", [B, 1])
        half = sb("half", [B, 2, S])
        half_of = sb("half_of", [B, 2])
        group = sb("group", [B, GROUPS])
        lab_i = sb("lab_i", [B, 1], I32)
        lab = sb("lab", [B, 4])
        onehot = sb("onehot", [B, NE])
        cnt = sb("cnt", [B, 2, NE])
        jobs_i = sb("jobs_i", [B, 2, NE], I32)
        jobs_f = sb("jobs_f", [B, 4, NE])
        slot_of = sb("slot_of", [B, NE + 1])
        in_slot = sb("in_slot", [B, NSLOT])
        row0 = sb("row0", [1, 6, NSLOT])
        cmp = sb("cmp", [1, JOBS, NE - 1])
        job_lab = sb("job_lab", [1, JOBS])
        slot_src = sb("slot_src", [1, NSLOT], I32)
        slot_dst = sb("slot_dst", [1, NSLOT], I32)
        job_exp = sb("job_exp", [1, JOBS], I32)
        g1_sb = sb("g1_sb", [P, K3 * DC, D]); g2_sb = sb("g2_sb", [P, DC, K3])
        e_first = sb("e_first", [B, D])
        gate_in = sb("gate_in", [B, K3, D])
        gate_T = sb("gate_T", [P, K3 * DC, B])
        gate_h = sb("gate_h", [P, DC, B])
        f_fac = sb("f_fac", [B, K3])
        lab_inv = sb("lab_inv", [B, NE + 1])
        logit = sb("logit", [B, K3]); lmax = sb("lmax", [B, 1])
        prob = sb("prob", [B, K3]); psum_ = sb("psum_", [B, 1]); prec = sb("prec", [B, 1])
        pw = sb("pw", [B, 3, K3])
        spread = sb("spread", [B, GROUPS, K3])
        w_tok = sb("w_tok", [P, GROUPS, K3])
        fac = sb("fac", [P, 2, TG, K3]); fac0 = sb("fac0", [P, TG, K3])

        def bank(name):
            return ctx.enter_context(nc.psum_tensor(name, [P, 512], F32))

        hid = [bank(f"hid{i}") for i in range(NP1)]
        accb = [bank(f"accb{i}") for i in range(4)]
        tr = [bank(f"tr{i}") for i in range(2)]

        x_loaded = [sem("x_loaded0"), sem("x_loaded1")]
        x_maxed, x_powed, x_cled, x_scaled = sem("x_maxed"), sem("x_powed"), sem("x_cled"), sem("x_scaled")
        x_hi_done, x_lo_done, x_turned, x_ready = sem("x_hi_done"), sem("x_lo_done"), sem("x_turned"), sem("x_ready")
        x_inv_done = sem("x_inv_done")
        f_loaded, f_step, f_scaled, f_hi_done, f_lo_done = sem("f_loaded"), sem("f_step"), sem("f_scaled"), sem("f_hi_done"), sem("f_lo_done")
        f_turned, f_ready = sem("f_turned"), sem("f_ready")
        w_loaded = [sem(f"w_loaded{i}") for i in range(STAGES)]
        w_maxed, w_reduced, w_powed, w_cled, w_scaled = sem("w_maxed"), sem("w_reduced"), sem("w_powed"), sem("w_cled"), sem("w_scaled")
        w_hi_done, w_lo_done, w_inv_done, pair_done = sem("w_hi_done"), sem("w_lo_done"), sem("w_inv_done"), sem("pair_done")
        hid_full, h_hi_done, h_lo_done, h_used = sem("hid_full"), sem("h_hi_done"), sem("h_lo_done"), sem("h_used")
        acc_drained = sem("acc_drained")
        e_stored = [sem("e_stored0"), sem("e_stored1")]
        w_now_done = sem("w_now_done")
        const_step, const_done = sem("const_step"), sem("const_done")
        lab_loaded, lab_step, lab_pe, meta_done = sem("lab_loaded"), sem("lab_step"), sem("lab_pe"), sem("meta_done")
        g_loaded, ef_loaded = sem("g_loaded"), sem("ef_loaded")
        gate_dve, gate_pe, gate_act = sem("gate_dve"), sem("gate_pe"), sem("gate_act")
        t0_loaded = sem("t0_loaded")
        en_loaded = [sem("en_loaded0"), sem("en_loaded1")]
        fac_done, base_done, combined = sem("fac_done"), sem("base_done"), sem("combined")
        t0_step = sem("t0_step")
        stored = [sem("stored0"), sem("stored1")]

        block = ctx.enter_context(nc.Block())

        x_rows = x.rearrange("(t g h) s d -> t (h s) g d", g=TG, h=2)
        out_rows = out.rearrange("(t g h) s d -> t (h s) g d", g=TG, h=2)
        e_rows = scratch[0:B].rearrange("(t g h) s d -> t (h s) g d", g=TG, h=2)
        x_first = x[:, 0, :]
        e_first_rows = scratch[0:B, 0, :]

        w_src = []
        for k in range(NSH):
            w_src += [(swi[k], 0, w_sh[:, k]), (swo[k], 1, w_sh[:, k])]
        for k in range(NE):
            w_src += [(wi[k], 0, w_exp[:, k]), (wo[k], 1, w_exp[:, k])]

        def parts(w, second):
            o = 2 * WCOL * second
            return w[:, o:o + WCOL], w[:, o + WCOL:o + 2 * WCOL]

        @block.sync
        def _(sp):
            def need(s, v):
                if not isinstance(v, int) or v > 0:
                    sp.wait_ge(s, v)

            def load_weight(w):
                src, second, _ = w_src[w]
                if w >= STAGES:
                    sp.wait_ge(w_lo_done, w - STAGES + 1)
                v = src.rearrange("(c p) n -> p c n", p=P)
                dst = stage[w % STAGES].rearrange("p (c n) -> p c n", n=v.shape[2])
                sp.dma_start(dst, v).then_inc(w_loaded[w % STAGES], 16)

            def load_tile(u, n, par):
                need(x_lo_done, n - 1)
                sp.dma_start(x_nat[:, par], one(x_rows, u)).then_inc(x_loaded[par], 16)

            def one(rows, u):
                return rows[u] if isinstance(u, int) else rows[bass.ds(u, 1)].rearrange("o p g d -> (o p) g d")

            def load_slots(t, par):
                need(x_lo_done, e_x(t) - 1)
                for j in range(SLOTS):
                    b = sp.value_load(slot_src[0:1, bass.ds(SLOTS * t + j, 1)], min_val=0, max_val=B - 1)
                    sp.dma_start(x_nat[S * (j % 2):S * (j % 2) + S, par, j // 2, :],
                                 x[bass.ds(b, 1)].rearrange("o s d -> (o s) d")).then_inc(x_loaded[par], 16)

            def store_slots(t, par):
                sp.wait_ge(acc_drained, e_drained(t))
                for j in range(SLOTS):
                    r = sp.value_load(slot_dst[0:1, bass.ds(SLOTS * t + j, 1)], min_val=0, max_val=B + NSLOT - 1)
                    sp.dma_start(scratch[bass.ds(r, 1)].rearrange("o s d -> (o s) d"),
                                 e_out[S * (j % 2):S * (j % 2) + S, par, j // 2, :]).then_inc(e_stored[par], 16)

            load_tile(0, 0, 0)
            load_weight(0)
            load_weight(1)
            sp.dma_start(lab_i[:, :], labels.rearrange("(b o) -> b o", o=1)).then_inc(lab_loaded, 16)
            load_weight(2)
            load_weight(3)
            sp.dma_start(f_nat[:, :], x_first).then_inc(f_loaded, 16)
            load_weight(4)
            sp.dma_start(g1_sb[:, :, :], g1.rearrange("(c p) n -> p c n", p=P)).then_inc(g_loaded, 16)
            sp.dma_start(g2_sb[:, :, :], g2.rearrange("(c p) n -> p c n", p=P)).then_inc(g_loaded, 16)
            for w in range(5, 9):
                load_weight(w)
            sp.wait_ge(meta_done, 1)
            load_slots(0, 1)
            load_slots(1, 0)
            for w in range(9, NW):
                load_weight(w)

            load_slots(2, 1)

            with sp.Fori(0, (JOBS - 3) // 2) as pair:
                t = 2 * pair + 1
                load_slots(t + 2, 0)
                store_slots(t - 1, 0)
                load_slots(t + 3, 1)
                store_slots(t, 1)
            t = JOBS - 2
            load_tile(1, b_x(1), b_x(1) % 2)
            store_slots(t - 1, 0)
            load_tile(2, b_x(2), b_x(2) % 2)
            store_slots(t, 1)
            store_slots(t + 1, 0)
            sp.wait_ge(e_stored[0], 16 * SLOTS * ((JOBS + 1) // 2))
            sp.wait_ge(e_stored[1], 16 * SLOTS * (JOBS // 2))
            sp.dma_start(e_first[:, :], e_first_rows).then_inc(ef_loaded, 16)
            sp.wait_ge(h_used, STEP_B)
            sp.dma_start(e_nat[1], e_rows[1]).then_inc(en_loaded[1], 16)
            sp.dma_start(x_t0, x_rows[0]).then_inc(t0_loaded, 16)
            sp.dma_start(e_t0, e_rows[0]).then_inc(t0_loaded, 16)
            sp.dma_start(e_nat[0], e_rows[2]).then_inc(en_loaded[0], 16)

            def tile_io(u, par, n_stored, more_x, more_e):
                sp.wait_ge(combined, 2 * (u - 1))
                sp.dma_start(one(out_rows, u - 1), acc[1 - par]).then_inc(stored[1 - par], 16)
                if more_e:
                    sp.dma_start(e_nat[1 - par], one(e_rows, u + 1)).then_inc(en_loaded[1 - par], 16)
                if more_x:
                    sp.wait_ge(base_done, u)
                    sp.dma_start(x_nat[:, b_x(par) % 2], one(x_rows, u + 2)).then_inc(x_loaded[b_x(par) % 2], 16)

            sp.wait_ge(base_done, 1)
            load_tile(3, b_x(3), b_x(3) % 2)
            sp.wait_ge(t0_step, K3 + 1)
            sp.dma_start(out_rows[0], x_t0).then_inc(stored[0], 16)
            with sp.Fori(0, 2) as pair:
                u = 2 * pair + 2
                tile_io(u, 0, None, True, True)
                tile_io(u + 1, 1, None, True, True)
            tile_io(6, 0, None, False, True)
            tile_io(7, 1, None, False, False)
            sp.wait_ge(combined, 2 * 7)
            sp.dma_start(out_rows[7], acc[1]).then_inc(stored[1], 16)
            sp.wait_ge(stored[0], 16 * 4)
            sp.wait_ge(stored[1], 16 * 4)

        @block.gpsimd
        def _(pool):
            n = [0]

            def ordered(ins):
                n[0] += 1
                ins.then_inc(const_step, 1)
                pool.wait_ge(const_step, n[0])

            ordered(pool.memset(identf[:, :], 0.0))
            pool.affine_select(out=identf[:, :], in_=identf[:, :], compare_op=ALU.not_equal, fill=1.0, base=0,
                               pattern=[[-1, P]], channel_multiplier=1).then_inc(const_done, 1)
            pool.wait_ge(const_done, 1)
            pool.tensor_copy(ident[:, :], identf[:, :]).then_inc(const_done, 1)

            def reduce_weight(w):
                pool.wait_ge(w_maxed, w + 1)
                pool.partition_all_reduce(w_all[:, w:w + 1], w_max[:, w:w + 1], P, ABSMAX).then_inc(w_reduced, 1)

            reduce_weight(0)
            ordered(pool.memset(ones[:, :], 1.0))
            pool.affine_select(out=lower[:, :], in_=ones[:, :], compare_op=ALU.is_gt, fill=0.0, base=0,
                               pattern=[[1, B]], channel_multiplier=-1).then_inc(const_done, 1)
            pool.iota(slot_no[:, :], [[1, NSLOT]], base=0, channel_multiplier=0,
                      allow_small_or_imprecise_dtypes=True).then_inc(const_done, 1)
            pool.iota(label_no[:, :], [[1, NE]], base=0, channel_multiplier=0,
                      allow_small_or_imprecise_dtypes=True).then_inc(const_done, 1)
            pool.iota(job_no[:, :, :], [[1, JOBS], [0, NE - 1]], base=0, channel_multiplier=0,
                      allow_small_or_imprecise_dtypes=True).then_inc(const_done, 1)
            pool.iota(batch_no[:, :], [[0, 1]], base=0, channel_multiplier=1,
                      allow_small_or_imprecise_dtypes=True).then_inc(const_done, 1)
            reduce_weight(1)
            ordered(pool.memset(group[:, :], 1.0))
            ordered(pool.affine_select(out=group[:, :], in_=group[:, :], compare_op=ALU.is_ge, fill=0.0, base=0,
                                       pattern=[[-2, GROUPS]], channel_multiplier=1))
            pool.affine_select(out=group[:, :], in_=group[:, :], compare_op=ALU.is_ge, fill=0.0, base=1,
                               pattern=[[2, GROUPS]], channel_multiplier=-1).then_inc(const_done, 1)
            for w in range(2, NW):
                reduce_weight(w)

        @block.tensor
        def _(pe):
            def need(s, v):
                if not isinstance(v, int) or v > 0:
                    pe.wait_ge(s, v)

            def hidden(s, f, w, rhs, n):
                need(h_lo_done, s - NP1 + 1)
                whi, wlo = parts(w, 0)
                for c in range(DC):
                    o = c * F + f * P
                    for i, (a, m) in enumerate(((whi, 0), (whi, 1), (wlo, 0))):
                        mm = pe.matmul(hid[f % NP1][:, 0:n], a[:, o:o + P], rhs(m, c),
                                       start=(c == 0 and i == 0), stop=(c == DC - 1 and i == 2))
                mm.then_inc(hid_full, 1)

            def project(s, f, w, groups, size, banks, wait=None):
                need(h_lo_done, s + 1)
                if f == 0 and wait is not None:
                    need(*wait)
                whi, wlo = parts(w, 1)
                r = f % RING
                for g in range(groups):
                    o = accb[banks[g // 2]][0:size, (g % 2) * D:(g % 2) * D + D]
                    hh, hl = h_hi[:, r, g * P:g * P + size], h_lo[:, r, g * P:g * P + size]
                    for i, (a, b) in enumerate(((hh, whi), (hh, wlo), (hl, whi))):
                        mm = pe.matmul(o, a, b[:, f * D:f * D + D], start=(f == 0 and i == 0 and g % 2 == 0),
                                       stop=(f == FC - 1 and i == 2), skip_group_check=True)
                mm.then_inc(h_used, 1)

            def turn(n, groups, fixed=0):
                pe.wait_ge(x_lo_done, n + 1)
                need(x_ready, n)
                width = groups * P
                for m, src in enumerate((x_hi, x_lo)):
                    b = tr[m if groups == TG else 0][:, :].bitcast(F16)
                    o = 0 if groups == TG else m * DC * width
                    for c in range(DC):
                        for g in range(groups):
                            at = o + c * width + g * P
                            mm = pe.transpose(b[:, at:at + P], src[:, g, c * P:(c + 1) * P], ident[:, :])
                mm.then_inc(x_turned, 1)

            def tile_rhs(par, n):
                return lambda m, c: x_T[:, par, m, c, 0:n]

            class Tail:
                owed = []

            def step(s, f, w, rhs, n, proj):
                hidden(s, f, w, rhs, n)
                Tail.owed.append(proj)
                if len(Tail.owed) > LAG:
                    Tail.owed.pop(0)()

            def shared_steps(s0, par, waits, extra):
                for k in range(NSH):
                    for f in range(FC):
                        q = k * FC + f
                        if f == 0 and k < len(waits.get("w", [])):
                            pe.wait_ge(w_lo_done, waits["w"][k])
                        step(s0 + q, f, w_sh[:, k], tile_rhs(par, TOK), TOK,
                             lambda q=q, k=k, f=f: project(s0 + q, f, w_sh[:, k], TG, P, (2 * k, 2 * k + 1),
                                                           waits.get(k)))
                        for fn in extra.get(q, ()):
                            fn()

            def expert_steps(t, par, extra):
                pe.wait_ge(x_ready, e_x(t) + 1)
                pe.wait_ge(w_now_done, 4 * (t + 1))
                w = w_now[par]
                for f in range(FC):
                    step(e_step(t) + f, f, w, tile_rhs(1 - par, ETOK), ETOK,
                         lambda f=f: project(e_step(t) + f, f, w, EG, P, (2 + par,), (acc_drained, e_drained(t) - 2)))
                    for fn in extra.get(f, ()):
                        fn()

            pe.wait_ge(const_done, 2)
            turn(0, TG)

            def count_labels():
                pe.wait_ge(const_done, 7)
                pe.wait_ge(lab_step, 5)
                pe.wait_ge(x_ready, 1)
                pe.matmul(tr[0][0:B, 0:NE], ones[:, :], onehot[:, :], start=True, stop=True)
                pe.matmul(tr[0][0:B, 64:64 + NE], lower[:, :], onehot[:, :], start=True, stop=True).then_inc(lab_pe, 1)

            def invert_slots():
                pe.wait_ge(lab_step, 16)
                pe.matmul(tr[0][0:1, 0:NSLOT], batch_no[:, :], in_slot[:, :], start=True, stop=True)
                pe.matmul(tr[0][0:1, 128:128 + NSLOT], ones[:, 0:1], in_slot[:, :], start=True, stop=True).then_inc(lab_pe, 1)

            def turn_first():
                pe.wait_ge(f_lo_done, 1)
                b = tr[1][:, :].bitcast(F16)
                for m, src in enumerate((f_hi, f_lo)):
                    for c in range(DC):
                        at = (m * DC + c) * B
                        mm = pe.transpose(b[:, at:at + B], src[:, c * P:(c + 1) * P], ident[0:B, 0:B])
                mm.then_inc(f_turned, 1)

            def turn_job0():
                pe.wait_ge(lab_step, 22)
                turn(1, EG)

            pe.wait_ge(x_ready, 1)
            shared_steps(0, 0, {"w": (1, 3), 0: (w_lo_done, 2), 1: (w_lo_done, 4)},
                         {0: (count_labels,), 3: (invert_slots,), 9: (turn_first,), 12: (turn_job0,)})

            pe.wait_ge(f_ready, 1)
            for k in range(NSH):
                for f in range(FC):
                    q = STEP_M + k * FC + f
                    step(q, f, w_sh[:, k], lambda m, c: f_T[:, m, c, :], B,
                         lambda q=q, k=k, f=f: project(q, f, w_sh[:, k], 1, B, (k,), (acc_drained, 1)))

            def next_job(t):
                return {5: (lambda: turn(e_x(t + 1), EG),)}

            expert_steps(0, 0, next_job(0))
            with pe.Fori(0, (JOBS - 3) // 2) as pair:
                t = 2 * pair + 1
                Tail.owed = [lambda q=q: project(e_step(t - 1) + q, q, w_now[0], EG, P, (2,)) for q in (FC - 2, FC - 1)]
                expert_steps(t, 1, next_job(t))
                expert_steps(t + 1, 0, next_job(t + 1))
            t = JOBS - 2
            Tail.owed = [lambda q=q: project(e_step(t - 1) + q, q, w_now[0], EG, P, (2,)) for q in (FC - 2, FC - 1)]
            expert_steps(t, 1, next_job(t))
            expert_steps(t + 1, 0, {5: (lambda: turn(b_x(1), TG),)})

            def turn_gate():
                pe.wait_ge(gate_dve, 2)
                pe.wait_ge(acc_drained, 4)
                pe.wait_ge(x_ready, b_x(1) + 1)
                for j in range(K3 * DC):
                    mm = pe.transpose(tr[0][:, j * B:(j + 1) * B],
                                      gate_in[:, j // DC, (j % DC) * P:(j % DC + 1) * P], identf[0:B, 0:B])
                mm.then_inc(gate_pe, 1)

            def gate_hidden():
                pe.wait_ge(gate_dve, 3)
                pe.wait_ge(g_loaded, 32)
                for m in range(DC):
                    for j in range(K3 * DC):
                        mm = pe.matmul(tr[1][:, m * B:(m + 1) * B], g1_sb[:, j, m * P:(m + 1) * P], gate_T[:, j, :],
                                       start=(j == 0), stop=(j == K3 * DC - 1))
                mm.then_inc(gate_pe, 1)

            def gate_logits():
                pe.wait_ge(gate_dve, 4)
                for m in range(DC):
                    mm = pe.matmul(tr[0][0:B, 0:K3], gate_h[:, m, :], g2_sb[:, m, :], start=(m == 0), stop=(m == DC - 1))
                mm.then_inc(gate_pe, 1)

            def gate_tokens():
                pe.wait_ge(gate_dve, 11)
                pe.matmul(tr[1][:, 0:GROUPS * K3], half[:, :, :].rearrange("b h s -> b (h s)"),
                          spread[:, :, :].rearrange("b g k -> b (g k)"), start=True, stop=True).then_inc(gate_pe, 1)

            def tile_steps(u, par, extra):
                pe.wait_ge(x_ready, b_x(u) + 1)
                first = isinstance(u, int) and u == 1
                w0 = (acc_drained, 4) if first else (combined, 2 * (u - 1) - 1)
                w1 = (acc_drained, e_drained(JOBS - 1)) if first else (combined, 2 * (u - 1))
                shared_steps(b_step(u), par, {0: w0, 1: w1}, extra)

            def next_tile(u):
                return {10: (lambda: turn(b_x(u + 1), TG),)}

            def owed_shared(s0):
                return [lambda q=q: project(s0 + q, q % FC, w_sh[:, NSH - 1], TG, P, (2, 3)) for q in (SH - 2, SH - 1)]

            xp = b_x(1) % 2
            tile_steps(1, xp, {4: (turn_gate,), 5: (gate_hidden,), 6: (gate_logits,), 9: (gate_tokens,),
                               12: (lambda: (pe.wait_ge(gate_dve, 12), turn(b_x(2), TG)),)})
            with pe.Fori(0, 2) as pair:
                u = 2 * pair + 2
                Tail.owed = owed_shared(b_step(u - 1))
                tile_steps(u, 1 - xp, next_tile(u))
                tile_steps(u + 1, xp, next_tile(u + 1))
            Tail.owed = owed_shared(b_step(5))
            tile_steps(6, 1 - xp, next_tile(6))
            tile_steps(7, xp, {})
            while Tail.owed:
                Tail.owed.pop(0)()

        @block.scalar
        def _(act):
            def need(s, v):
                if not isinstance(v, int) or v > 0:
                    act.wait_ge(s, v)

            def relu_hi(s, f, n):
                act.wait_ge(hid_full, s + 1)
                need(h_used, s - RING + 1)
                act.activation(h_hi[:, f % RING, 0:n], hid[f % NP1][:, 0:n], ACT.Relu).then_inc(h_hi_done, 1)

            def x_split(n, par, groups):
                act.wait_ge(x_scaled, n + 1)
                need(x_turned, n)
                for g in range(groups):
                    a = act.activation(x_hi[:, g, :], x_nat[:, par, g, :], ACT.Copy, scale=x_scale[:, g:g + 1])
                a.then_inc(x_hi_done, 1)

            def x_keep(n, par, groups):
                act.wait_ge(x_turned, n + 1)
                if groups == TG:
                    for m in range(2):
                        a = act.activation(x_T[:, par, m, :, :], tr[m][:, :].bitcast(F16).rearrange("p (c t) -> p c t", c=DC),
                                           ACT.Copy)
                else:
                    a = act.activation(x_T[:, par, :, :, 0:ETOK],
                                       tr[0][:, :].bitcast(F16).rearrange("p (m c t) -> p m c t", m=2, c=DC), ACT.Copy)
                a.then_inc(x_ready, 1)

            def w_split(w):
                act.wait_ge(w_scaled, w + 1)
                _, second, dst = w_src[w]
                act.activation(parts(dst, second)[0], stage[w % STAGES], ACT.Copy,
                               scale=w_scale[:, w:w + 1]).then_inc(w_hi_done, 1)

            def steps(s0, count, n, extra):
                for q in range(count):
                    relu_hi(s0 + q, q, n)
                    for fn in extra.get(q, ()):
                        fn()

            x_split(0, 0, TG)
            x_keep(0, 0, TG)
            w_split(0)
            w_split(1)

            def drain_t0(k):
                act.wait_ge(h_used, (k + 1) * FC)
                for h in range(2):
                    a = act.activation(s_t0[:, k, 2 * h:2 * h + 2, :],
                                       accb[2 * k + h][:, :].rearrange("p (g d) -> p g d", d=D), ACT.Copy)
                a.then_inc(acc_drained, 1)

            def f_split():
                act.wait_ge(f_scaled, 1)
                act.activation(f_hi[:, :], f_nat[:, :], ACT.Copy, scale=f_scale[:, 0:1]).then_inc(f_hi_done, 1)

            def f_keep():
                act.wait_ge(f_turned, 1)
                act.activation(f_T[:, :, :, :].rearrange("p m c b -> p (m c b)"),
                               tr[1][:, :].bitcast(F16)[:, 0:2 * DC * B], ACT.Copy).then_inc(f_ready, 1)

            extra = {q: [] for q in range(SH)}
            for w in range(2, NW):
                extra[W_AT[w]].append(lambda w=w: w_split(w))
            extra[5].append(f_split)
            extra[10].append(f_keep)
            extra[10].append(lambda: x_split(1, 1, EG))
            extra[13].append(lambda: x_keep(1, 1, EG))
            extra[10].append(lambda: drain_t0(0))
            steps(0, SH, TOK, extra)

            def drain_first(k):
                act.wait_ge(h_used, STEP_M + (k + 1) * FC)
                act.wait_ge(f_step, F_FAC)
                act.activation(gate_in[:, 1 + k, :], accb[k][0:B, 0:D], ACT.Copy,
                               scale=f_fac[:, 1 + k:2 + k]).then_inc(acc_drained, 1)

            steps(STEP_M, SH, B, {1: (lambda: drain_t0(1),), FC + 2: (lambda: drain_first(0),)})

            def drain_job(t, par):
                act.wait_ge(h_used, e_step(t + 1))
                if not isinstance(t, int) or t >= 2:
                    act.wait_ge(e_stored[par], 16 * SLOTS * stored_before(t, par))
                act.activation(e_out[:, par].rearrange("p g d -> p (g d)"), accb[2 + par][:, :],
                               ACT.Copy).then_inc(acc_drained, 1)

            def stored_before(t, par):
                return t // 2 if isinstance(t, int) else (t - par) // 2

            def job(t, par, drain, split, keep):
                steps(e_step(t), FC, ETOK, {1: (drain,), 3: (split,), 6: (keep,)})

            def next_split(t, par):
                return (lambda: x_split(e_x(t + 1), par, EG)), (lambda: x_keep(e_x(t + 1), par, EG))

            job(0, 0, lambda: drain_first(1), *next_split(0, 0))
            job(1, 1, lambda: drain_job(0, 0), *next_split(1, 1))
            job(2, 0, lambda: drain_job(1, 1), *next_split(2, 0))
            with act.Fori(0, (JOBS - 5) // 2) as pair:
                t = 2 * pair + 3
                job(t, 1, lambda: drain_job(t - 1, 0), *next_split(t, 1))
                job(t + 1, 0, lambda: drain_job(t, 1), *next_split(t + 1, 0))
            t = JOBS - 2
            job(t, 1, lambda: drain_job(t - 1, 0), *next_split(t, 1))
            n = b_x(1)
            job(t + 1, 0, lambda: drain_job(t, 1), lambda: x_split(n, n % 2, TG), lambda: x_keep(n, n % 2, TG))

            def softmax_exp():
                act.wait_ge(gate_dve, 6)
                act.activation(prob[:, :], logit[:, :], ACT.Exp, bias=lmax[:, 0:1]).then_inc(gate_act, 1)

            def tile(u, par, extra, more=True):
                m = dict(extra)
                if more:
                    n = b_x(u + 1)
                    m.setdefault(6, ()); m.setdefault(11, ())
                    at_keep = 14 if isinstance(u, int) and u == 1 else 11
                    m[6] = m[6] + (lambda: x_split(n, par, TG),)
                    m[at_keep] = m.get(at_keep, ()) + (lambda: x_keep(n, par, TG),)
                steps(b_step(u), SH, TOK, m)

            xp = b_x(1) % 2
            tile(1, 1 - xp, {1: (lambda: drain_job(JOBS - 1, 0),), 8: (softmax_exp,)})
            with act.Fori(0, 2) as pair:
                u = 2 * pair + 2
                tile(u, xp, {})
                tile(u + 1, 1 - xp, {})
            tile(6, xp, {})
            tile(7, 1 - xp, {}, more=False)

        @block.vector
        def _(dve):
            def need(s, v):
                if not isinstance(v, int) or v > 0:
                    dve.wait_ge(s, v)

            MASK = 0x7F800000
            FLOOR = float(27 << 23)
            ITOP = float(256 << 23)

            def h_low(s, f, n):
                dve.wait_ge(h_hi_done, s + 1)
                dve.scalar_tensor_tensor(out=h_lo[:, f % RING, 0:n], in0=hid[f % NP1][:, 0:n], scalar=0.0,
                                         in1=h_hi[:, f % RING, 0:n], op0=ALU.max, op1=ALU.subtract).then_inc(h_lo_done, 1)

            def x_measure(n, par, groups, loads, inv):
                dve.wait_ge(x_loaded[par], loads)
                dve.tensor_reduce(x_max[:, 0:groups], x_nat[:, par, 0:groups, :], AX.X, ALU.max,
                                  apply_absolute_value=True).then_inc(x_maxed, 1)
                dve.wait_ge(x_maxed, n + 1)
                dve.tensor_scalar(x_pow[:, 0:groups].bitcast(I32), x_max[:, 0:groups].bitcast(I32), MASK, None,
                                  ALU.bitwise_and).then_inc(x_powed, 1)
                dve.wait_ge(x_powed, n + 1)
                dve.tensor_scalar(x_cl[:, 0:groups].bitcast(I32), x_pow[:, 0:groups].bitcast(I32), FLOOR, None,
                                  ALU.max).then_inc(x_cled, 1)
                dve.wait_ge(x_cled, n + 1)
                dve.tensor_scalar(x_scale[:, 0:groups].bitcast(I32), x_cl[:, 0:groups].bitcast(I32), -1.0, ITOP,
                                  ALU.mult, ALU.add).then_inc(x_scaled, 1)
                if inv is not None:
                    dve.tensor_scalar(inv, x_cl[:, :], 0.25, None, ALU.mult).then_inc(x_inv_done, 1)

            def x_low(n, par, groups):
                dve.wait_ge(x_hi_done, n + 1)
                for g in range(groups):
                    i = dve.scalar_tensor_tensor(out=x_lo[:, g, :], in0=x_nat[:, par, g, :], scalar=x_scale[:, g:g + 1],
                                                 in1=x_hi[:, g, :], op0=ALU.mult, op1=ALU.subtract)
                i.then_inc(x_lo_done, 1)

            def w_measure(w):
                dve.wait_ge(w_loaded[w % STAGES], 16 * (w // STAGES + 1))
                dve.tensor_reduce(w_max[:, w:w + 1], stage[w % STAGES], AX.X, ALU.max,
                                  apply_absolute_value=True).then_inc(w_maxed, 1)

            def w_scales(w):
                dve.wait_ge(w_reduced, w + 1)
                c = slice(w, w + 1)
                dve.tensor_scalar(w_pow[:, c].bitcast(I32), w_all[:, c].bitcast(I32), MASK, None,
                                  ALU.bitwise_and).then_inc(w_powed, 1)
                dve.wait_ge(w_powed, w + 1)
                dve.tensor_scalar(w_cl[:, c].bitcast(I32), w_pow[:, c].bitcast(I32), FLOOR, None,
                                  ALU.max).then_inc(w_cled, 1)
                dve.wait_ge(w_cled, w + 1)
                dve.tensor_scalar(w_scale[:, c].bitcast(I32), w_cl[:, c].bitcast(I32), -1.0, ITOP,
                                  ALU.mult, ALU.add).then_inc(w_scaled, 1)

            def w_low(w):
                dve.wait_ge(w_hi_done, w + 1)
                dve.wait_ge(w_scaled, w + 1)
                _, second, dst = w_src[w]
                hi, lo = parts(dst, second)
                dve.scalar_tensor_tensor(out=lo, in0=stage[w % STAGES], scalar=w_scale[:, w:w + 1], in1=hi,
                                         op0=ALU.mult, op1=ALU.subtract).then_inc(w_lo_done, 1)

            def steps(s0, count, n, extra):
                for q in range(count):
                    h_low(s0 + q, q, n)
                    for fn in extra.get(q, ()):
                        fn()

            x_measure(0, 0, TG, 16, x_inv0[:, :])
            w_measure(0)
            x_low(0, 0, TG)
            w_scales(0)
            w_measure(1)
            w_low(0)
            w_scales(1)
            w_measure(2)
            w_low(1)

            n_lab = [0]

            def lab_op(ins):
                n_lab[0] += 1
                ins.then_inc(lab_step, 1)
                dve.wait_ge(lab_step, n_lab[0])

            def labels_in():
                dve.wait_ge(lab_loaded, 16)
                dve.wait_ge(const_done, 7)
                lab_op(dve.tensor_copy(lab[:, 0:1], lab_i[:, :]))
                lab_op(dve.tensor_scalar(lab[:, 1:2], lab[:, 0:1], 0.0, float(NE), ALU.is_lt, ALU.mult))
                lab_op(dve.tensor_tensor(lab[:, 2:3], lab[:, 0:1], lab[:, 1:2], ALU.add))
                lab_op(dve.tensor_scalar(lab[:, 3:4], lab[:, 2:3], 0.0, float(NE - 1), ALU.max, ALU.min))
                lab_op(dve.tensor_scalar(onehot[:, :], label_no[:, :], lab[:, 3:4], None, ALU.is_equal))

            def place_slots():
                dve.wait_ge(lab_pe, 1)
                lab_op(dve.tensor_scalar(jobs_i[:, 0, :], tr[0][0:B, 0:NE], float(SLOTS - 1), None, ALU.add))
                lab_op(dve.tensor_scalar(jobs_i[:, 1, :], jobs_i[:, 0, :], 2, None, ALU.logical_shift_right))
                lab_op(dve.tensor_copy(jobs_f[:, 0, :], jobs_i[:, 1, :]))
                lab_op(dve.tensor_copy(cnt[:, 1, :], tr[0][0:B, 64:64 + NE]))
                lab_op(dve.tensor_tensor_scan(jobs_f[:, 1, :], ones[:, 0:NE], jobs_f[:, 0, :], 0.0, ALU.mult, ALU.add))
                lab_op(dve.tensor_tensor(jobs_f[:, 2, :], jobs_f[:, 1, :], jobs_f[:, 0, :], ALU.subtract))
                lab_op(dve.scalar_tensor_tensor(out=jobs_f[:, 3, :], in0=jobs_f[:, 2, :], scalar=float(SLOTS),
                                                in1=cnt[:, 1, :], op0=ALU.mult, op1=ALU.add))
                lab_op(dve.tensor_tensor(slot_of[:, 0:NE], jobs_f[:, 3, :], onehot[:, :], ALU.mult))
                lab_op(dve.tensor_reduce(slot_of[:, NE:NE + 1], slot_of[:, 0:NE], AX.X, ALU.add))
                lab_op(dve.tensor_scalar(slot_no2[:, :], slot_no[0:1, :], float(B), None, ALU.add))
                lab_op(dve.tensor_scalar(in_slot[:, :], slot_no[:, :], slot_of[:, NE:NE + 1], None, ALU.is_equal))

            slot_no2 = row0[:, 0, :]

            def name_slots():
                dve.wait_ge(lab_pe, 2)
                lab_op(dve.tensor_tensor(row0[:, 1, :], tr[0][0:1, 128:128 + NSLOT], slot_no2, ALU.mult))
                lab_op(dve.tensor_tensor(row0[:, 2, :], tr[0][0:1, 0:NSLOT], slot_no2, ALU.add))
                lab_op(dve.tensor_copy(slot_src[:, :], tr[0][0:1, 0:NSLOT]))
                lab_op(dve.tensor_tensor(row0[:, 3, :], row0[:, 2, :], row0[:, 1, :], ALU.subtract))
                lab_op(dve.tensor_copy(slot_dst[:, :], row0[:, 3, :]))
                lab_op(dve.tensor_tensor(cmp[:, :, :], job_no[:, :, :],
                                         jobs_f[0:1, 2:3, 1:NE].to_broadcast([1, JOBS, NE - 1]), ALU.is_ge))
                lab_op(dve.tensor_reduce(job_lab[:, :], cmp[:, :, :], AX.X, ALU.add))
                dve.tensor_copy(job_exp[:, :], job_lab[:, :]).then_inc(meta_done, 1)

            n_f = [0]

            def f_op(ins):
                n_f[0] += 1
                ins.then_inc(f_step, 1)
                dve.wait_ge(f_step, n_f[0])

            def f_measure():
                dve.wait_ge(f_loaded, 16)
                f_op(dve.tensor_reduce(f_max[:, :], f_nat[:, :], AX.X, ALU.max, apply_absolute_value=True))
                f_op(dve.tensor_scalar(f_pow[:, :].bitcast(I32), f_max[:, :].bitcast(I32), MASK, None, ALU.bitwise_and))
                f_op(dve.tensor_scalar(f_cl[:, :].bitcast(I32), f_pow[:, :].bitcast(I32), FLOOR, None, ALU.max))
                dve.tensor_scalar(f_scale[:, :].bitcast(I32), f_cl[:, :].bitcast(I32), -1.0, ITOP,
                                  ALU.mult, ALU.add).then_inc(f_scaled, 1)
                f_op(dve.tensor_scalar(f_inv[:, :], f_cl[:, :], 0.25, None, ALU.mult))

            def f_low():
                dve.wait_ge(f_hi_done, 1)
                dve.wait_ge(f_scaled, 1)
                dve.scalar_tensor_tensor(out=f_lo[:, :], in0=f_nat[:, :], scalar=f_scale[:, 0:1], in1=f_hi[:, :],
                                         op0=ALU.mult, op1=ALU.subtract).then_inc(f_lo_done, 1)

            def undo_scales():
                dve.wait_ge(w_cled, NW)
                f_op(dve.tensor_scalar(w_inv[:, :, :], w_cl[:, :].rearrange("p (n o) -> p n o", o=2), 0.25, None, ALU.mult))
                f_op(dve.tensor_tensor(pair_inv[:, :], w_inv[:, :, 0], w_inv[:, :, 1], ALU.mult))
                f_op(dve.tensor_tensor(lab_inv[:, 0:NE], onehot[:, :], pair_inv[0:B, NSH:NSH + NE], ALU.mult))
                f_op(dve.tensor_reduce(lab_inv[:, NE:NE + 1], lab_inv[:, 0:NE], AX.X, ALU.add))
                f_op(dve.tensor_scalar(f_fac[:, 0:1], lab_inv[:, NE:NE + 1], f_inv[:, 0:1], None, ALU.mult))
                f_op(dve.tensor_scalar(f_fac[:, 1:K3], pair_inv[0:B, 0:NSH], f_inv[:, 0:1], None, ALU.mult))
                f_op(dve.tensor_reduce(half_of[:, :], identf[0:B, 0:B].rearrange("b (g j) -> b j g", j=2), AX.X, ALU.add))
                f_op(dve.tensor_copy(half[:, :, :], half_of[:, :].rearrange("b (j o) -> b j o", o=1).to_broadcast([B, 2, S])))
                assert n_f[0] == F_FAC

            def w_unit(w):
                w_scales(w)
                if w + 1 < NW:
                    w_measure(w + 1)
                w_low(w)

            def load_expert(t, par, part):
                if part == 0:
                    if isinstance(t, int) and t < 2:
                        dve.wait_ge(w_lo_done, NW)
                    else:
                        dve.wait_ge(h_used, e_step(t - 1))
                e = dve.value_load(job_exp[0:1, bass.ds(t, 1)], min_val=0, max_val=NE - 1)
                src = w_exp[:, bass.ds(e, 1), part * WCOL:(part + 1) * WCOL].rearrange("p o n -> p (o n)")
                dve.tensor_copy(w_now[par][:, part * WCOL:(part + 1) * WCOL], src).then_inc(w_now_done, 1)

            extra = {q: [] for q in range(SH)}
            for w in range(2, NW):
                extra[W_AT[w]].append(lambda w=w: w_unit(w))
            labels_in()
            extra[1].append(place_slots)
            extra[4].append(name_slots)
            extra[4].append(f_measure)
            extra[6].append(f_low)
            extra[9].append(lambda: x_measure(1, 1, EG, 16 * SLOTS, None))
            extra[11].append(lambda: x_low(1, 1, EG))
            steps(0, SH, TOK, extra)
            steps(STEP_M, SH, B, {
                0: (undo_scales,),
                **{2 + i: (lambda i=i: (dve.wait_ge(meta_done, 1), load_expert(0, 0, i)),) for i in range(4)},
            })

            def job(t, par, tail=None):
                nxt = t + 1
                ex = {}
                if tail is None:
                    cnt_ = 16 + 16 * SLOTS * ((nxt + 1) // 2) if par == 0 else 16 * SLOTS * (nxt // 2 + 1)
                    ex[1] = [lambda: x_measure(e_x(nxt), par, EG, cnt_, None)]
                    ex[3] = [lambda: x_low(e_x(nxt), par, EG)]
                    for i, q in enumerate((2, 4, 5, 6)):
                        ex.setdefault(q, []).append(lambda i=i: load_expert(nxt, 1 - par, i))
                else:
                    ex = tail
                steps(e_step(t), FC, ETOK, ex)

            job(0, 0)
            with dve.Fori(0, (JOBS - 3) // 2) as pair:
                t = 2 * pair + 1
                job(t, 1)
                job(t + 1, 0)
            t = JOBS - 2
            job(t, 1)
            n = b_x(1)
            xp = n % 2
            loads_e = {0: 16 + 16 * SLOTS * (JOBS // 2), 1: 16 * SLOTS * ((JOBS + 1) // 2)}

            def tile_loads(u, par):
                first = 1 if par == xp else 2
                return loads_e[par] + 16 * ((u - first) // 2 + 1)

            job(t + 1, 0, {1: (lambda: x_measure(n, xp, TG, tile_loads(1, xp), x_inv[:, xp, :]),),
                           3: (lambda: x_low(n, xp, TG),)})

            n_g = [0]

            def g_op(ins):
                n_g[0] += 1
                ins.then_inc(gate_dve, 1)
                dve.wait_ge(gate_dve, n_g[0])

            def gate_rows():
                dve.wait_ge(ef_loaded, 16)
                g_op(dve.tensor_scalar(gate_in[:, 0, :], e_first[:, :], f_fac[:, 0:1], None, ALU.mult))
                g_op(dve.tensor_copy(pw[:, 0, 0:1], lab_inv[:, NE:NE + 1]))

            def gate_turned():
                dve.wait_ge(gate_pe, 1)
                g_op(dve.tensor_copy(gate_T[:, :, :].rearrange("p j b -> p (j b)"), tr[0][:, 0:K3 * DC * B]))

            def gate_relu():
                dve.wait_ge(gate_pe, 2)
                g_op(dve.tensor_scalar(gate_h[:, :, :].rearrange("p m b -> p (m b)"), tr[1][:, 0:DC * B], 0.0, None, ALU.max))

            def gate_max():
                dve.wait_ge(gate_pe, 3)
                g_op(dve.tensor_copy(logit[:, :], tr[0][0:B, 0:K3]))
                g_op(dve.tensor_reduce(lmax[:, :], logit[:, :], AX.X, ALU.max, negate=True))

            def gate_soft():
                dve.wait_ge(const_done, 8)
                dve.wait_ge(gate_act, 1)
                g_op(dve.tensor_reduce(psum_[:, :], prob[:, :], AX.X, ALU.add))
                g_op(dve.reciprocal(prec[:, :], psum_[:, :]))
                g_op(dve.tensor_copy(pw[:, 0, 1:K3], pair_inv[0:B, 0:NSH]))
                g_op(dve.scalar_tensor_tensor(out=pw[:, 1, :], in0=prob[:, :], scalar=prec[:, 0:1], in1=pw[:, 0, :],
                                              op0=ALU.mult, op1=ALU.mult))
                g_op(dve.tensor_tensor(spread[:, :, :],
                                       group[:, :].rearrange("b (g o) -> b g o", o=1).to_broadcast([B, GROUPS, K3]),
                                       pw[:, 1:2, :].to_broadcast([B, GROUPS, K3]), ALU.mult))

            def gate_out():
                dve.wait_ge(gate_pe, 4)
                g_op(dve.tensor_copy(w_tok[:, :, :].rearrange("p g k -> p (g k)"), tr[1][:, 0:GROUPS * K3]))

            def base(u, par, inv, n_en):
                dve.wait_ge(x_inv_done, u + 1)
                dve.tensor_tensor(fac[:, par], one_tile(u), inv, ALU.mult).then_inc(fac_done, 1)
                dve.wait_ge(fac_done, u)
                dve.wait_ge(en_loaded[par], n_en)
                need(stored[par], stored_need(u, par))
                xb = b_x(par) % 2
                for g in range(TG):
                    i = dve.scalar_tensor_tensor(out=acc[par][:, g, :], in0=e_nat[par][:, g, :], scalar=fac[:, par, g, 0:1],
                                                 in1=x_nat[:, xb, g, :], op0=ALU.mult, op1=ALU.add)
                i.then_inc(base_done, 1)

            def stored_need(u, par):
                return 16 * ((u - 1) // 2) if par else 16 * (u // 2)

            def one_tile(u):
                return w_tok[:, TG * u:TG * (u + 1), :] if isinstance(u, int) else w_tok[:, bass.ds(TG * u, TG), :]

            def combine(u, par, k):
                dve.wait_ge(h_used, b_step(u) + (k + 1) * FC)
                if k == 0:
                    dve.wait_ge(base_done, u)
                else:
                    dve.wait_ge(combined, 2 * u - 1)
                for g in range(TG):
                    i = dve.scalar_tensor_tensor(out=acc[par][:, g, :], in0=accb[2 * k + g // 2][:, (g % 2) * D:(g % 2 + 1) * D],
                                                 scalar=fac[:, par, g, 1 + k:2 + k], in1=acc[par][:, g, :],
                                                 op0=ALU.mult, op1=ALU.add)
                i.then_inc(combined, 1)

            def inv_of(par):
                xb = b_x(par) % 2
                return x_inv[:, xb, :].rearrange("p (g o) -> p g o", o=1).to_broadcast([P, TG, K3])

            n_t0 = [0]

            def t0_base():
                dve.wait_ge(t0_loaded, 32)
                dve.tensor_tensor(fac0[:, :, :], w_tok[:, 0:TG, :],
                                  x_inv0[:, :].rearrange("p (g o) -> p g o", o=1).to_broadcast([P, TG, K3]),
                                  ALU.mult).then_inc(t0_step, 1)
                dve.wait_ge(t0_step, 1)

            def t0_term(k):
                rows = e_t0 if k == 0 else s_t0[:, k - 1]
                if k == K3 - 1:
                    dve.wait_ge(acc_drained, 2)
                for g in range(TG):
                    i = dve.scalar_tensor_tensor(out=x_t0[:, g, :], in0=rows[:, g, :], scalar=fac0[:, g, k:k + 1],
                                                 in1=x_t0[:, g, :], op0=ALU.mult, op1=ALU.add)
                i.then_inc(t0_step, 1)
                dve.wait_ge(t0_step, k + 2)

            def tile(u, par, extra, n_next=None):
                m = {q: tuple(v) for q, v in extra.items()}
                if n_next is not None:
                    xb = b_x(par + 1) % 2
                    m[5] = m.get(5, ()) + (lambda: x_measure(b_x(u + 1), xb, TG, n_next, x_inv[:, xb, :]),)
                    m[7] = m.get(7, ()) + (lambda: x_low(b_x(u + 1), xb, TG),)
                steps(b_step(u), SH, TOK, m)

            def en_count(u, par):
                return 16 * ((u + 1) // 2) if par else 16 * (u // 2)

            def usual(u, par):
                return {1: (lambda: combine(u - 1, 1 - par, 1),), 3: (lambda: base(u, par, inv_of(par), en_count(u, par)),),
                        9: (lambda: combine(u, par, 0),)}

            tile(1, 1, {4: (gate_rows,), 5: (gate_turned,), 6: (gate_relu,), 7: (gate_max,), 8: (gate_soft,), 10: (gate_out,),
                        11: (lambda: base(1, 1, inv_of(1), 16),), 12: (lambda: combine(1, 1, 0),),
                        13: (t0_base, lambda: t0_term(0)), 14: (lambda: t0_term(1),),
                        15: (lambda: t0_term(2),)}, tile_loads(2, 1 - xp))
            with dve.Fori(0, 2) as pair:
                u = 2 * pair + 2
                tile(u, 0, usual(u, 0), tile_loads(u + 1, xp))
                tile(u + 1, 1, usual(u + 1, 1), tile_loads(u + 2, 1 - xp))
            tile(6, 0, usual(6, 0), tile_loads(7, xp))
            tile(7, 1, usual(7, 1))
            combine(7, 1, 1)


F_FAC = 12
W_AT = [None, None] + [0, 1, 3, 4, 5, 7, 8, 9, 11, 12, 13, 14]


_INS = ['x', 'itok_B_0_2', 'L0_cond_wi', 'L0_cond_wo', 'L0_cond_swi', 'L0_cond_swo', 'L0_cond_g1', 'L0_cond_g2']


def kernel(**inputs):
    import numpy as _np
    import concourse.bacc as _bacc
    from concourse import mybir as _mybir
    from concourse.bass_utils import run_bass_kernel_spmd as _run

    nc = _bacc.Bacc("TRN2", target_bir_lowering=False, num_devices=1)
    arrays, args = {}, []
    for name in _INS:
        a = _np.ascontiguousarray(inputs[name])
        arrays[f"in_{name}_dram"] = a
        args.append(nc.dram_tensor(f"in_{name}_dram", a.shape, _mybir.dt.from_np(a.dtype), kind="ExternalInput").ap())
    shape = inputs['x'].shape
    args.append(nc.dram_tensor("out_0_dram", shape, _mybir.dt.float32, kind="ExternalOutput").ap())
    build(nc, *args)
    r = _run(nc, [arrays], core_ids=[0])
    return r.results[0]["out_0_dram"]
```

```python
from contextlib import ExitStack

import concourse.bass as bass
from concourse import mybir

F32 = mybir.dt.float32
F16 = mybir.dt.float16
I32 = mybir.dt.int32
ALU = mybir.AluOpType
ACT = mybir.ActivationFunctionType
AX = mybir.AxisListType
ABSMAX = bass.bass_isa.ReduceOp.absmax

P = 128



def build(nc, x, labels, wi, wo, swi, swo, g1, g2, out):
    B, S, D = x.shape
    NE, _, F = wi.shape
    NSH = swi.shape[0]
    DC = D // P
    FC = F // P
    TG = 4
    TOK = TG * P
    TILES = B * S // TOK
    SLOTS = 4
    EG = SLOTS * S // P
    ETOK = SLOTS * S
    JOBS = (B + NE * (SLOTS - 1)) // SLOTS
    NSLOT = JOBS * SLOTS
    GROUPS = B * S // P
    PERTILE = TOK // S
    K3 = 1 + NSH
    WCOL = DC * F
    assert WCOL == FC * D and S == 64 and JOBS % 2 == 1 and TILES == 8 and B <= P

    LAG, RING, NP1 = 3, 4, 2
    SH = NSH * FC
    EARLY = 2
    STEP_M = EARLY * SH
    STEP_E = STEP_M + SH
    STEP_B = STEP_E + FC * JOBS

    def e_step(t):
        return STEP_E + FC * t

    def b_step(u):
        return STEP_B + SH * (u - EARLY)

    def e_x(t):
        return EARLY + t

    def b_x(u):
        return JOBS + u

    def e_drained(t):
        return NSH * (EARLY + 1) + t + 1

    def b_combined(u, k):
        return NSH * (u - EARLY) + k + 1

    NW = 2 * NSH + 2 * NE
    STAGES = 4

    ctx = ExitStack()
    with ctx:
        def sb(name, shape, dt=F32):
            return ctx.enter_context(nc.sbuf_tensor(name, shape, dt))

        def sem(name):
            return ctx.enter_context(nc.semaphore(name))

        scratch = nc.dram_tensor("expert_rows", (B + NSLOT, S, D), F32, kind="Internal").ap()

        w_exp = sb("w_exp", [P, NE, 4 * WCOL], F16)
        w_sh = sb("w_sh", [P, NSH, 4 * WCOL], F16)
        region = sb("region", [P, 4 * WCOL], F32)
        stage = [region[:, s * WCOL:(s + 1) * WCOL] for s in range(STAGES)]
        w_now = [region[:, 2 * s * WCOL:2 * (s + 1) * WCOL].bitcast(F16) for s in range(2)]
        rg = region[:, :].rearrange("p (b g d) -> p b g d", g=TG, d=D)
        e_nat = [rg[:, i] for i in range(2)]
        acc = [rg[:, 2 + i] for i in range(2)]
        x_early = [rg[:, 4 + 2 * i] for i in range(EARLY)]
        e_early = [rg[:, 5 + 2 * i] for i in range(EARLY)]
        x_nat = sb("x_nat", [P, 2, TG, D])
        x_hi = sb("x_hi", [P, TG, D], F16)
        x_lo = sb("x_lo", [P, TG, D], F16)
        x_T = sb("x_T", [P, 2, 2, DC, TOK], F16)
        h_hi = sb("h_hi", [P, RING, TOK], F16)
        h_lo = sb("h_lo", [P, RING, TOK], F16)
        e_out = sb("e_out", [P, 2, EG, D])
        s_early = sb("s_early", [P, EARLY, NSH, TG, D])
        f_nat = sb("f_nat", [B, D])
        f_hi = sb("f_hi", [B, D], F16)
        f_lo = sb("f_lo", [B, D], F16)
        f_T = sb("f_T", [P, 2, DC, B], F16)
        x_max = sb("x_max", [P, TG]); x_pow = sb("x_pow", [P, TG]); x_cl = sb("x_cl", [P, TG])
        x_scale = sb("x_scale", [P, TG])
        x_inv = sb("x_inv", [P, 2, TG]); x_inv_early = sb("x_inv_early", [P, EARLY, TG])
        f_max = sb("f_max", [B, 1]); f_pow = sb("f_pow", [B, 1]); f_cl = sb("f_cl", [B, 1])
        f_scale = sb("f_scale", [B, 1]); f_inv = sb("f_inv", [B, 1])
        w_max = sb("w_max", [P, NW]); w_all = sb("w_all", [P, NW]); w_pow = sb("w_pow", [P, NW])
        w_cl = sb("w_cl", [P, NW])
        w_scale = sb("w_scale", [P, NW])
        w_inv = sb("w_inv", [P, NW // 2, 2])
        pair_inv = sb("pair_inv", [P, NW // 2])
        identf = sb("identf", [P, P]); ident = sb("ident", [P, P], F16)
        ones = sb("ones", [B, B])
        lower = sb("lower", [B, B])
        slot_no = sb("slot_no", [B, NSLOT])
        label_no = sb("label_no", [B, NE])
        job_no = sb("job_no", [1, JOBS, NE - 1])
        batch_no = sb("batch_no", [B, 1])
        half = sb("half", [B, 2, S])
        half_of = sb("half_of", [B, 2])
        group = sb("group", [B, GROUPS])
        lab_i = sb("lab_i", [B, 1], I32)
        lab = sb("lab", [B, 4])
        onehot = sb("onehot", [B, NE])
        cnt = sb("cnt", [B, 2, NE])
        jobs_i = sb("jobs_i", [B, 2, NE], I32)
        jobs_f = sb("jobs_f", [B, 4, NE])
        slot_of = sb("slot_of", [B, NE + 1])
        in_slot = sb("in_slot", [B, NSLOT])
        row0 = sb("row0", [1, 6, NSLOT])
        cmp = sb("cmp", [1, JOBS, NE - 1])
        job_lab = sb("job_lab", [1, JOBS])
        slot_src = sb("slot_src", [1, NSLOT], I32)
        slot_dst = sb("slot_dst", [1, NSLOT], I32)
        job_exp = sb("job_exp", [1, JOBS], I32)
        late = w_exp[:, 0].bitcast(F32)
        g1_sb = late[:, 0:K3 * DC * D].rearrange("p (j n) -> p j n", n=D)
        o = K3 * DC * D
        e_first = late[0:B, o:o + D]
        o += D
        gate_T = late[:, o:o + K3 * DC * B].rearrange("p (j b) -> p j b", b=B)
        o += K3 * DC * B
        gate_h = late[:, o:o + DC * B].rearrange("p (m b) -> p m b", b=B)
        g2_sb = sb("g2_sb", [P, DC, K3])
        gate_in = sb("gate_in", [B, K3, D])
        f_fac = sb("f_fac", [B, K3])
        lab_inv = sb("lab_inv", [B, NE + 1])
        logit = sb("logit", [B, K3]); lmax = sb("lmax", [B, 1])
        prob = sb("prob", [B, K3]); psum_ = sb("psum_", [B, 1]); prec = sb("prec", [B, 1])
        pw = sb("pw", [B, 3, K3])
        spread = sb("spread", [B, GROUPS, K3])
        w_tok = sb("w_tok", [P, GROUPS, K3])
        fac = sb("fac", [P, 2, TG, K3]); fac_early = sb("fac_early", [P, EARLY, TG, K3])

        def bank(name):
            return ctx.enter_context(nc.psum_tensor(name, [P, 512], F32))

        hid = [bank(f"hid{i}") for i in range(NP1)]
        accb = [bank(f"accb{i}") for i in range(4)]
        tr = [bank(f"tr{i}") for i in range(2)]

        x_loaded = [sem("x_loaded0"), sem("x_loaded1")]
        x_maxed, x_powed, x_cled, x_scaled = sem("x_maxed"), sem("x_powed"), sem("x_cled"), sem("x_scaled")
        x_hi_done, x_lo_done, x_turned, x_ready = sem("x_hi_done"), sem("x_lo_done"), sem("x_turned"), sem("x_ready")
        x_inv_done = sem("x_inv_done")
        f_loaded, f_step, f_scaled, f_hi_done, f_lo_done = sem("f_loaded"), sem("f_step"), sem("f_scaled"), sem("f_hi_done"), sem("f_lo_done")
        f_turned, f_ready = sem("f_turned"), sem("f_ready")
        w_loaded = [sem(f"w_loaded{i}") for i in range(STAGES)]
        w_maxed, w_reduced, w_powed, w_cled, w_scaled = sem("w_maxed"), sem("w_reduced"), sem("w_powed"), sem("w_cled"), sem("w_scaled")
        w_hi_done, w_lo_done, w_squared = sem("w_hi_done"), sem("w_lo_done"), sem("w_squared")
        w_hi_half, w_lo_half, x_hi_turned = sem("w_hi_half"), sem("w_lo_half"), sem("x_hi_turned")
        hid_full, h_hi_done, h_lo_done, h_used = sem("hid_full"), sem("h_hi_done"), sem("h_lo_done"), sem("h_used")
        acc_drained = sem("acc_drained")
        e_stored = [sem("e_stored0"), sem("e_stored1")]
        w_now_done = sem("w_now_done")
        const_step, const_done = sem("const_step"), sem("const_done")
        lab_loaded, lab_step, lab_pe, meta_done = sem("lab_loaded"), sem("lab_step"), sem("lab_pe"), sem("meta_done")
        g_loaded, ef_loaded = sem("g_loaded"), sem("ef_loaded")
        gate_dve, gate_pe, gate_act = sem("gate_dve"), sem("gate_pe"), sem("gate_act")
        early_loaded = sem("early_loaded")
        en_loaded = [sem("en_loaded0"), sem("en_loaded1")]
        fac_done, base_done, combined = sem("fac_done"), sem("base_done"), sem("combined")
        early_step, early_stored = sem("early_step"), sem("early_stored")
        stored = [sem("stored0"), sem("stored1")]

        block = ctx.enter_context(nc.Block())

        x_rows = x.rearrange("(t g h) s d -> t (h s) g d", g=TG, h=2)
        out_rows = out.rearrange("(t g h) s d -> t (h s) g d", g=TG, h=2)
        e_rows = scratch[0:B].rearrange("(t g h) s d -> t (h s) g d", g=TG, h=2)
        x_first = x[:, 0, :]
        e_first_rows = scratch[0:B, 0, :]

        w_src = []
        for k in range(NSH):
            w_src += [(swi[k], 0, w_sh[:, k]), (swo[k], 1, w_sh[:, k])]
        for k in range(NE):
            w_src += [(wi[k], 0, w_exp[:, k]), (wo[k], 1, w_exp[:, k])]

        def parts(w, second):
            o = 2 * WCOL * second
            return w[:, o:o + WCOL], w[:, o + WCOL:o + 2 * WCOL]

        def pieces(w, cols):
            v = cols.rearrange("p (c n) -> p c n", c=2)
            return (v[:, 0, :], v[:, 1, :]) if w_src[w][1] else (v[:, :, 0:F // 2], v[:, :, F // 2:F])

        @block.sync
        def _(sp):
            def need(s, v):
                if not isinstance(v, int) or v > 0:
                    sp.wait_ge(s, v)

            def load_weight(w):
                src, second, _ = w_src[w]
                if w >= STAGES:
                    sp.wait_ge(w_lo_done, w - STAGES + 1)
                v = src.rearrange("(c p) n -> p c n", p=P)
                dst = stage[w % STAGES].rearrange("p (c n) -> p c n", n=v.shape[2])
                sp.dma_start(dst, v).then_inc(w_loaded[w % STAGES], 16)

            def load_tile(u, n, par):
                need(x_lo_done, n - 1)
                sp.dma_start(x_nat[:, par], x_rows[u]).then_inc(x_loaded[par], 16)

            def load_slots(t, par):
                need(x_lo_done, e_x(t) - 1)
                for j in range(SLOTS):
                    b = sp.value_load(slot_src[0:1, bass.ds(SLOTS * t + j, 1)], min_val=0, max_val=B - 1)
                    sp.dma_start(x_nat[S * (j % 2):S * (j % 2) + S, par, j // 2, :],
                                 x[bass.ds(b, 1)].rearrange("o s d -> (o s) d")).then_inc(x_loaded[par], 16)

            def store_slots(t, par):
                sp.wait_ge(acc_drained, e_drained(t))
                for j in range(SLOTS):
                    r = sp.value_load(slot_dst[0:1, bass.ds(SLOTS * t + j, 1)], min_val=0, max_val=B + NSLOT - 1)
                    sp.dma_start(scratch[bass.ds(r, 1)].rearrange("o s d -> (o s) d"),
                                 e_out[S * (j % 2):S * (j % 2) + S, par, j // 2, :]).then_inc(e_stored[par], 16)

            load_tile(0, 0, 0)
            load_weight(0)
            load_weight(1)
            load_weight(2)
            load_weight(3)
            sp.dma_start(lab_i[:, :], labels.rearrange("(b o) -> b o", o=1)).then_inc(lab_loaded, 16)
            load_tile(1, 1, 1)
            sp.dma_start(f_nat[:, :], x_first).then_inc(f_loaded, 16)
            sp.dma_start(g2_sb[:, :, :], g2.rearrange("(c p) n -> p c n", p=P)).then_inc(g_loaded, 16)
            for w in range(STAGES, 10):
                load_weight(w)
            sp.wait_ge(meta_done, 1)
            load_slots(0, 0)
            load_slots(1, 1)
            for w in range(10, NW):
                load_weight(w)

            load_slots(2, 0)

            with sp.Fori(0, (JOBS - 3) // 2) as pair:
                t = 2 * pair + 1
                load_slots(t + 2, 1)
                store_slots(t - 1, 0)
                load_slots(t + 3, 0)
                store_slots(t, 1)
            t = JOBS - 2
            for i in range(2):
                load_tile(EARLY + i, b_x(EARLY + i), b_x(EARLY + i) % 2)
                store_slots(t - 1 + i, i)
            sp.wait_ge(w_now_done, 4 * JOBS)
            sp.dma_start(g1_sb, g1.rearrange("(c p) n -> p c n", p=P)).then_inc(g_loaded, 16)
            store_slots(t + 1, 0)
            sp.wait_ge(e_stored[0], 16 * SLOTS * ((JOBS + 1) // 2))
            sp.wait_ge(e_stored[1], 16 * SLOTS * (JOBS // 2))
            sp.dma_start(e_first, e_first_rows).then_inc(ef_loaded, 16)
            sp.wait_ge(h_used, STEP_B)
            for i in range(2):
                sp.dma_start(e_nat[i], e_rows[EARLY + i]).then_inc(en_loaded[i], 16)
            for i in range(EARLY):
                sp.dma_start(x_early[i], x_rows[i]).then_inc(early_loaded, 16)
                sp.dma_start(e_early[i], e_rows[i]).then_inc(early_loaded, 16)

            def store_tile(u):
                sp.wait_ge(combined, b_combined(u, NSH - 1))
                sp.dma_start(out_rows[u], acc[u % 2]).then_inc(stored[u % 2], 16)

            for u in range(EARLY, TILES):
                if u > EARLY:
                    store_tile(u - 1)
                    if u + 1 < TILES:
                        sp.wait_ge(stored[(u - 1) % 2], 16 * ((u - 1 - EARLY) // 2 + 1))
                        sp.dma_start(e_nat[(u + 1) % 2], e_rows[u + 1]).then_inc(en_loaded[(u + 1) % 2], 16)
                if u + 2 < TILES:
                    sp.wait_ge(base_done, u - EARLY + 1)
                    load_tile(u + 2, b_x(u + 2), b_x(u + 2) % 2)
            for i in range(EARLY):
                sp.wait_ge(early_step, EARLY + K3 * (i + 1))
                sp.dma_start(out_rows[i], x_early[i]).then_inc(early_stored, 16)
            store_tile(TILES - 1)
            sp.wait_ge(early_stored, 16 * EARLY)
            for i in range(2):
                sp.wait_ge(stored[i], 16 * (TILES - EARLY) // 2)

        @block.gpsimd
        def _(pool):
            n = [0]

            def ordered(ins):
                n[0] += 1
                ins.then_inc(const_step, 1)
                pool.wait_ge(const_step, n[0])

            ordered(pool.memset(identf[:, :], 0.0))
            pool.affine_select(out=identf[:, :], in_=identf[:, :], compare_op=ALU.not_equal, fill=1.0, base=0,
                               pattern=[[-1, P]], channel_multiplier=1).then_inc(const_done, 1)
            pool.wait_ge(const_done, 1)
            pool.tensor_copy(ident[:, :], identf[:, :]).then_inc(const_done, 1)

            def reduce_weight(w):
                if w in DVE_MEASURES:
                    pool.wait_ge(w_maxed, measured(w))
                else:
                    pool.wait_ge(w_squared, measured(w))
                pool.partition_all_reduce(w_all[:, w:w + 1], w_max[:, w:w + 1], P, ABSMAX).then_inc(w_reduced, 1)

            reduce_weight(0)
            ordered(pool.memset(ones[:, :], 1.0))
            pool.affine_select(out=lower[:, :], in_=ones[:, :], compare_op=ALU.is_gt, fill=0.0, base=0,
                               pattern=[[1, B]], channel_multiplier=-1).then_inc(const_done, 1)
            pool.iota(slot_no[:, :], [[1, NSLOT]], base=0, channel_multiplier=0,
                      allow_small_or_imprecise_dtypes=True).then_inc(const_done, 1)
            pool.iota(label_no[:, :], [[1, NE]], base=0, channel_multiplier=0,
                      allow_small_or_imprecise_dtypes=True).then_inc(const_done, 1)
            pool.iota(job_no[:, :, :], [[1, JOBS], [0, NE - 1]], base=0, channel_multiplier=0,
                      allow_small_or_imprecise_dtypes=True).then_inc(const_done, 1)
            pool.iota(batch_no[:, :], [[0, 1]], base=0, channel_multiplier=1,
                      allow_small_or_imprecise_dtypes=True).then_inc(const_done, 1)
            reduce_weight(1)
            ordered(pool.memset(group[:, :], 1.0))
            ordered(pool.affine_select(out=group[:, :], in_=group[:, :], compare_op=ALU.is_ge, fill=0.0, base=0,
                                       pattern=[[-2, GROUPS]], channel_multiplier=1))
            pool.affine_select(out=group[:, :], in_=group[:, :], compare_op=ALU.is_ge, fill=0.0, base=1,
                               pattern=[[2, GROUPS]], channel_multiplier=-1).then_inc(const_done, 1)
            for w in range(2, NW):
                reduce_weight(w)

        @block.tensor
        def _(pe):
            def need(s, v):
                if not isinstance(v, int) or v > 0:
                    pe.wait_ge(s, v)

            def hidden(s, f, w, rhs, n):
                need(h_lo_done, s - NP1 + 1)
                whi, wlo = parts(w, 0)
                for c in range(DC):
                    o = c * F + f * P
                    for i, (a, m) in enumerate(((whi, 0), (whi, 1), (wlo, 0))):
                        mm = pe.matmul(hid[f % NP1][:, 0:n], a[:, o:o + P], rhs(m, c),
                                       start=(c == 0 and i == 0), stop=(c == DC - 1 and i == 2))
                mm.then_inc(hid_full, 1)

            def project(s, f, w, groups, size, banks, wait=None, split=()):
                need(h_lo_done, s + 1)
                if f == 0 and wait is not None:
                    need(*wait)
                for which, count in split:
                    pe.wait_ge(which, count)
                whi, wlo = parts(w, 1)
                r = f % RING
                for g in range(groups):
                    o = accb[banks[g // 2]][0:size, (g % 2) * D:(g % 2) * D + D]
                    hh, hl = h_hi[:, r, g * P:g * P + size], h_lo[:, r, g * P:g * P + size]
                    for i, (a, b) in enumerate(((hh, whi), (hh, wlo), (hl, whi))):
                        mm = pe.matmul(o, a, b[:, f * D:f * D + D], start=(f == 0 and i == 0 and g % 2 == 0),
                                       stop=(f == FC - 1 and i == 2), skip_group_check=True)
                mm.then_inc(h_used, 1)

            def turn(n, groups, fixed=0):
                pe.wait_ge(x_lo_done, n + 1)
                need(x_ready, n)
                width = groups * P
                for m, src in enumerate((x_hi, x_lo)):
                    b = tr[m if groups == TG else 0][:, :].bitcast(F16)
                    o = 0 if groups == TG else m * DC * width
                    for c in range(DC):
                        for g in range(groups):
                            at = o + c * width + g * P
                            mm = pe.transpose(b[:, at:at + P], src[:, g, c * P:(c + 1) * P], ident[:, :])
                mm.then_inc(x_turned, 1)

            def tile_rhs(par, n):
                return lambda m, c: x_T[:, par, m, c, 0:n]

            class Tail:
                owed = []

            def step(s, f, w, rhs, n, proj):
                hidden(s, f, w, rhs, n)
                Tail.owed.append(proj)
                if len(Tail.owed) > LAG:
                    Tail.owed.pop(0)()

            def shared_steps(s0, par, waits, extra):
                for k in range(NSH):
                    for f in range(FC):
                        q = k * FC + f
                        for which, count in waits.get(("wi", q), ()):
                            pe.wait_ge(which, count)
                        step(s0 + q, f, w_sh[:, k], tile_rhs(par, TOK), TOK,
                             lambda q=q, k=k, f=f: project(s0 + q, f, w_sh[:, k], TG, P, (2 * k, 2 * k + 1),
                                                           waits.get(k), waits.get(("wo", q), ())))
                        for fn in extra.get(q, ()):
                            fn()

            def expert_steps(t, par, extra):
                pe.wait_ge(x_ready, e_x(t) + 1)
                pe.wait_ge(w_now_done, 4 * (t + 1))
                w = w_now[par]
                for f in range(FC):
                    step(e_step(t) + f, f, w, tile_rhs(par, ETOK), ETOK,
                         lambda f=f: project(e_step(t) + f, f, w, EG, P, (2 + par,), (acc_drained, e_drained(t) - 2)))
                    for fn in extra.get(f, ()):
                        fn()

            pe.wait_ge(const_done, 2)
            for m, (src, there, seen) in enumerate(((x_hi, x_hi_done, x_hi_turned), (x_lo, x_lo_done, x_turned))):
                pe.wait_ge(there, 1)
                for c in range(DC):
                    for g in range(TG):
                        at = c * TOK + g * P
                        mm = pe.transpose(tr[m][:, :].bitcast(F16)[:, at:at + P], src[:, g, c * P:(c + 1) * P],
                                          ident[:, :])
                mm.then_inc(seen, 1)

            def count_labels():
                pe.wait_ge(const_done, 7)
                pe.wait_ge(lab_step, 5)
                pe.wait_ge(x_ready, 1)
                pe.matmul(tr[0][0:B, 0:NE], ones[:, :], onehot[:, :], start=True, stop=True)
                pe.matmul(tr[0][0:B, 64:64 + NE], lower[:, :], onehot[:, :], start=True, stop=True).then_inc(lab_pe, 1)

            def invert_slots():
                pe.wait_ge(lab_step, 16)
                pe.matmul(tr[0][0:1, 0:NSLOT], batch_no[:, :], in_slot[:, :], start=True, stop=True)
                pe.matmul(tr[0][0:1, 128:128 + NSLOT], ones[:, 0:1], in_slot[:, :], start=True, stop=True).then_inc(lab_pe, 1)

            def turn_first():
                pe.wait_ge(f_lo_done, 1)
                pe.wait_ge(x_ready, 2)
                b = tr[1][:, :].bitcast(F16)
                for m, src in enumerate((f_hi, f_lo)):
                    for c in range(DC):
                        at = (m * DC + c) * B
                        mm = pe.transpose(b[:, at:at + B], src[:, c * P:(c + 1) * P], ident[0:B, 0:B])
                mm.then_inc(f_turned, 1)

            def turn_tile1():
                pe.wait_ge(lab_step, 22)
                turn(1, TG)

            def turn_job0():
                pe.wait_ge(f_ready, 1)
                turn(e_x(0), EG)

            pe.wait_ge(x_ready, 1)
            shared_steps(0, 0, {("wi", 0): ((w_lo_half, 1),), ("wi", FC // 2): ((w_lo_done, 1),),
                                ("wo", 0): ((w_lo_half, 2),), ("wo", FC // 2): ((w_lo_done, 2),),
                                ("wi", FC): ((w_lo_done, 3),), ("wo", FC): ((w_lo_done, 4),)},
                         {5: (count_labels,), 9: (invert_slots,), 13: (turn_tile1,)})
            pe.wait_ge(x_ready, 2)
            shared_steps(SH, 1, {0: (acc_drained, 1), 1: (acc_drained, 2)}, {4: (turn_first,), 13: (turn_job0,)})

            pe.wait_ge(f_ready, 1)
            for k in range(NSH):
                for f in range(FC):
                    q = STEP_M + k * FC + f
                    step(q, f, w_sh[:, k], lambda m, c: f_T[:, m, c, :], B,
                         lambda q=q, k=k, f=f: project(q, f, w_sh[:, k], 1, B, (k,), (acc_drained, NSH + 1)))

            def next_job(t):
                return {5: (lambda: turn(e_x(t + 1), EG),)}

            expert_steps(0, 0, next_job(0))
            with pe.Fori(0, (JOBS - 3) // 2) as pair:
                t = 2 * pair + 1
                Tail.owed = [lambda q=q: project(e_step(t - 1) + q, q, w_now[0], EG, P, (2,)) for q in range(FC - LAG, FC)]
                expert_steps(t, 1, next_job(t))
                expert_steps(t + 1, 0, next_job(t + 1))
            t = JOBS - 2
            Tail.owed = [lambda q=q: project(e_step(t - 1) + q, q, w_now[0], EG, P, (2,)) for q in range(FC - LAG, FC)]
            expert_steps(t, 1, next_job(t))
            expert_steps(t + 1, 0, {5: (lambda: turn(b_x(EARLY), TG),)})

            def turn_gate():
                pe.wait_ge(gate_dve, 2)
                pe.wait_ge(acc_drained, NSH * (EARLY + 1))
                pe.wait_ge(x_ready, b_x(EARLY) + 1)
                for j in range(K3 * DC):
                    mm = pe.transpose(tr[0][:, j * B:(j + 1) * B],
                                      gate_in[:, j // DC, (j % DC) * P:(j % DC + 1) * P], identf[0:B, 0:B])
                mm.then_inc(gate_pe, 1)

            def gate_hidden():
                pe.wait_ge(gate_dve, 3)
                pe.wait_ge(g_loaded, 32)
                for m in range(DC):
                    for j in range(K3 * DC):
                        mm = pe.matmul(tr[1][:, m * B:(m + 1) * B], g1_sb[:, j, m * P:(m + 1) * P], gate_T[:, j, :],
                                       start=(j == 0), stop=(j == K3 * DC - 1))
                mm.then_inc(gate_pe, 1)

            def gate_logits():
                pe.wait_ge(gate_dve, 4)
                for m in range(DC):
                    mm = pe.matmul(tr[0][0:B, 0:K3], gate_h[:, m, :], g2_sb[:, m, :], start=(m == 0), stop=(m == DC - 1))
                mm.then_inc(gate_pe, 1)

            def gate_tokens():
                pe.wait_ge(gate_dve, 11)
                pe.matmul(tr[1][:, 0:GROUPS * K3], half[:, :, :].rearrange("b h s -> b (h s)"),
                          spread[:, :, :].rearrange("b g k -> b (g k)"), start=True, stop=True).then_inc(gate_pe, 1)

            def tile_steps(u, par, extra):
                pe.wait_ge(x_ready, b_x(u) + 1)
                first = isinstance(u, int) and u == EARLY
                waits = {0: (acc_drained, NSH * (EARLY + 1)), 1: (acc_drained, e_drained(JOBS - 1))} if first else {
                    k: (combined, b_combined(u - 1, k)) for k in range(NSH)}
                shared_steps(b_step(u), par, waits, extra)

            def next_tile(u):
                return {10: (lambda: turn(b_x(u + 1), TG),)}

            def owed_shared(s0):
                return [lambda q=q: project(s0 + q, q % FC, w_sh[:, NSH - 1], TG, P, (2, 3)) for q in range(SH - LAG, SH)]

            xp = b_x(EARLY) % 2
            tile_steps(EARLY, xp, {6: (turn_gate,), 7: (gate_hidden,), 8: (gate_logits,), 11: (gate_tokens,),
                                   13: (lambda: (pe.wait_ge(gate_dve, 12), turn(b_x(EARLY + 1), TG)),)})
            with pe.Fori(0, (TILES - EARLY - 2) // 2) as pair:
                u = 2 * pair + EARLY + 1
                Tail.owed = owed_shared(b_step(u - 1))
                tile_steps(u, 1 - xp, next_tile(u))
                tile_steps(u + 1, xp, next_tile(u + 1))
            Tail.owed = owed_shared(b_step(TILES - 2))
            tile_steps(TILES - 1, 1 - xp, {})
            while Tail.owed:
                Tail.owed.pop(0)()

        @block.scalar
        def _(act):
            def need(s, v):
                if not isinstance(v, int) or v > 0:
                    act.wait_ge(s, v)

            def relu_hi(s, f, n):
                act.wait_ge(hid_full, s + 1)
                need(h_used, s - RING + 1)
                act.activation(h_hi[:, f % RING, 0:n], hid[f % NP1][:, 0:n], ACT.Relu).then_inc(h_hi_done, 1)

            def x_split(n, par, groups):
                act.wait_ge(x_scaled, n + 1)
                need(x_turned, n)
                for g in range(groups):
                    a = act.activation(x_hi[:, g, :], x_nat[:, par, g, :], ACT.Copy, scale=x_scale[:, g:g + 1])
                a.then_inc(x_hi_done, 1)

            def x_keep(n, par, groups):
                act.wait_ge(x_turned, n + 1)
                if groups == TG:
                    for m in range(2):
                        a = act.activation(x_T[:, par, m, :, :], tr[m][:, :].bitcast(F16).rearrange("p (c t) -> p c t", c=DC),
                                           ACT.Copy)
                else:
                    a = act.activation(x_T[:, par, :, :, 0:ETOK],
                                       tr[0][:, :].bitcast(F16).rearrange("p (m c t) -> p m c t", m=2, c=DC), ACT.Copy)
                a.then_inc(x_ready, 1)

            def w_split(w):
                act.wait_ge(w_scaled, w + 1)
                _, second, dst = w_src[w]
                act.activation(parts(dst, second)[0], stage[w % STAGES], ACT.Copy,
                               scale=w_scale[:, w:w + 1]).then_inc(w_hi_done, 1)

            def w_split_half(w, i):
                if i == 0:
                    act.wait_ge(w_scaled, w + 1)
                _, second, dst = w_src[w]
                act.activation(pieces(w, parts(dst, second)[0])[i], pieces(w, stage[w % STAGES])[i], ACT.Copy,
                               scale=w_scale[:, w:w + 1]).then_inc((w_hi_half, w_hi_done)[i], 1)

            def w_square(w):
                act.wait_ge(w_loaded[w % STAGES], 16 * (w // STAGES + 1))
                _, second, dst = w_src[w]
                act.activation(parts(dst, second)[1], stage[w % STAGES], ACT.Square,
                               accum_out=w_max[:, w:w + 1]).then_inc(w_squared, 1)

            def steps(s0, count, n, extra):
                for q in range(count):
                    relu_hi(s0 + q, q, n)
                    for fn in extra.get(q, ()):
                        fn()

            x_split(0, 0, TG)
            for m, seen in enumerate((x_hi_turned, x_turned)):
                if m == 1:
                    w_split_half(0, 0)
                act.wait_ge(seen, 1)
                a = act.activation(x_T[:, 0, m, :, :], tr[m][:, :].bitcast(F16).rearrange("p (c t) -> p c t", c=DC),
                                   ACT.Copy)
            a.then_inc(x_ready, 1)
            w_split_half(0, 1)

            def drain_early(i, k):
                act.wait_ge(h_used, i * SH + (k + 1) * FC)
                for h in range(2):
                    a = act.activation(s_early[:, i, k, 2 * h:2 * h + 2, :],
                                       accb[2 * k + h][:, :].rearrange("p (g d) -> p g d", d=D), ACT.Copy)
                a.then_inc(acc_drained, 1)

            def f_split():
                act.wait_ge(f_scaled, 1)
                act.activation(f_hi[:, :], f_nat[:, :], ACT.Copy, scale=f_scale[:, 0:1]).then_inc(f_hi_done, 1)

            def f_keep():
                act.wait_ge(f_turned, 1)
                act.activation(f_T[:, :, :, :].rearrange("p m c b -> p (m c b)"),
                               tr[1][:, :].bitcast(F16)[:, 0:2 * DC * B], ACT.Copy).then_inc(f_ready, 1)

            extra = {q: [] for q in range(EARLY * SH)}
            extra[0] += [lambda: w_split_half(1, 0), lambda: w_split_half(1, 1)]
            extra[10].append(lambda: x_split(1, 1, TG))
            extra[14].append(lambda: x_keep(1, 1, TG))
            for w in range(2, NW):
                if w not in DVE_MEASURES:
                    extra[W_AT[w] - 1].append(lambda w=w: w_square(w))
                extra[W_AT[w]].append(lambda w=w: w_split(w))
            extra[15].append(f_split)
            extra[16].append(lambda: drain_early(0, 0))
            extra[20].append(lambda: drain_early(0, 1))
            extra[21].append(f_keep)
            extra[21].append(lambda: x_split(e_x(0), 0, EG))
            extra[30].append(lambda: drain_early(1, 0))
            extra[31].append(lambda: x_keep(e_x(0), 0, EG))
            steps(0, EARLY * SH, TOK, extra)

            def drain_first(k):
                act.wait_ge(h_used, STEP_M + (k + 1) * FC)
                act.wait_ge(f_step, F_FAC)
                act.activation(gate_in[:, 1 + k, :], accb[k][0:B, 0:D], ACT.Copy,
                               scale=f_fac[:, 1 + k:2 + k]).then_inc(acc_drained, 1)

            steps(STEP_M, SH, B, {2: (lambda: drain_early(1, 1),), FC + 3: (lambda: drain_first(0),)})

            def drain_job(t, par):
                act.wait_ge(h_used, e_step(t + 1))
                if not isinstance(t, int) or t >= 2:
                    act.wait_ge(e_stored[par], 16 * SLOTS * stored_before(t, par))
                act.activation(e_out[:, par].rearrange("p g d -> p (g d)"), accb[2 + par][:, :],
                               ACT.Copy).then_inc(acc_drained, 1)

            def stored_before(t, par):
                return t // 2 if isinstance(t, int) else (t - par) // 2

            def job(t, par, drain, split, keep):
                steps(e_step(t), FC, ETOK, {2: (drain,), 3: (split,), 6: (keep,)})

            def next_split(t, par):
                return (lambda: x_split(e_x(t + 1), 1 - par, EG)), (lambda: x_keep(e_x(t + 1), 1 - par, EG))

            job(0, 0, lambda: drain_first(1), *next_split(0, 0))
            job(1, 1, lambda: drain_job(0, 0), *next_split(1, 1))
            job(2, 0, lambda: drain_job(1, 1), *next_split(2, 0))
            with act.Fori(0, (JOBS - 5) // 2) as pair:
                t = 2 * pair + 3
                job(t, 1, lambda: drain_job(t - 1, 0), *next_split(t, 1))
                job(t + 1, 0, lambda: drain_job(t, 1), *next_split(t + 1, 0))
            t = JOBS - 2
            job(t, 1, lambda: drain_job(t - 1, 0), *next_split(t, 1))
            n = b_x(EARLY)
            job(t + 1, 0, lambda: drain_job(t, 1), lambda: x_split(n, n % 2, TG), lambda: x_keep(n, n % 2, TG))

            def softmax_exp():
                act.wait_ge(gate_dve, 6)
                act.activation(prob[:, :], logit[:, :], ACT.Exp, bias=lmax[:, 0:1]).then_inc(gate_act, 1)

            def tile(u, par, extra, more=True):
                m = dict(extra)
                if more:
                    n = b_x(u + 1)
                    m.setdefault(6, ()); m.setdefault(11, ())
                    at_keep = 14 if isinstance(u, int) else 11
                    m[6] = m[6] + (lambda: x_split(n, par, TG),)
                    m[at_keep] = m.get(at_keep, ()) + (lambda: x_keep(n, par, TG),)
                steps(b_step(u), SH, TOK, m)

            xp = b_x(EARLY) % 2
            tile(EARLY, 1 - xp, {2: (lambda: drain_job(JOBS - 1, 0),), 10: (softmax_exp,)})
            with act.Fori(0, (TILES - EARLY - 2) // 2) as pair:
                u = 2 * pair + EARLY + 1
                tile(u, xp, {})
                tile(u + 1, 1 - xp, {})
            tile(TILES - 1, xp, {}, more=False)

        @block.vector
        def _(dve):
            def need(s, v):
                if not isinstance(v, int) or v > 0:
                    dve.wait_ge(s, v)

            MASK = 0x7F800000
            FLOOR = float(77 << 23)
            XTOP = float(255 << 23)
            WTOP = float(258 << 23)
            HALF = float(64 << 23)

            def h_low(s, f, n):
                dve.wait_ge(h_hi_done, s + 1)
                dve.scalar_tensor_tensor(out=h_lo[:, f % RING, 0:n], in0=hid[f % NP1][:, 0:n], scalar=0.0,
                                         in1=h_hi[:, f % RING, 0:n], op0=ALU.max, op1=ALU.subtract).then_inc(h_lo_done, 1)

            def x_measure(n, par, groups, loads, inv):
                dve.wait_ge(x_loaded[par], loads)
                dve.tensor_reduce(x_max[:, 0:groups], x_nat[:, par, 0:groups, :], AX.X, ALU.max,
                                  apply_absolute_value=True).then_inc(x_maxed, 1)
                dve.wait_ge(x_maxed, n + 1)
                dve.tensor_scalar(x_pow[:, 0:groups].bitcast(I32), x_max[:, 0:groups].bitcast(I32), MASK, None,
                                  ALU.bitwise_and).then_inc(x_powed, 1)
                dve.wait_ge(x_powed, n + 1)
                dve.tensor_scalar(x_cl[:, 0:groups].bitcast(I32), x_pow[:, 0:groups].bitcast(I32), FLOOR, None,
                                  ALU.max).then_inc(x_cled, 1)
                dve.wait_ge(x_cled, n + 1)
                dve.tensor_scalar(x_scale[:, 0:groups].bitcast(I32), x_cl[:, 0:groups].bitcast(I32), -1.0, XTOP,
                                  ALU.mult, ALU.add).then_inc(x_scaled, 1)
                if inv is not None:
                    dve.tensor_scalar(inv, x_cl[:, :], 0.5, None, ALU.mult).then_inc(x_inv_done, 1)

            def x_low(n, par, groups, between=None):
                dve.wait_ge(x_hi_done, n + 1)
                for g in range(groups):
                    if between is not None and g == 3:
                        between()
                    i = dve.scalar_tensor_tensor(out=x_lo[:, g, :], in0=x_nat[:, par, g, :], scalar=x_scale[:, g:g + 1],
                                                 in1=x_hi[:, g, :], op0=ALU.mult, op1=ALU.subtract)
                i.then_inc(x_lo_done, 1)

            def w_measure(w):
                dve.wait_ge(w_loaded[w % STAGES], 16 * (w // STAGES + 1))
                dve.tensor_reduce(w_max[:, w:w + 1], stage[w % STAGES], AX.X, ALU.max,
                                  apply_absolute_value=True).then_inc(w_maxed, 1)

            def w_scales(w):
                dve.wait_ge(w_reduced, w + 1)
                c = slice(w, w + 1)
                if w not in DVE_MEASURES:
                    dve.tensor_scalar(w_pow[:, c].bitcast(I32), w_all[:, c].bitcast(I32), 1, MASK,
                                      ALU.logical_shift_right, ALU.bitwise_and).then_inc(w_powed, 1)
                else:
                    dve.tensor_scalar(w_pow[:, c].bitcast(I32), w_all[:, c].bitcast(I32), MASK, None,
                                      ALU.bitwise_and).then_inc(w_powed, 1)
                dve.wait_ge(w_powed, w + 1)
                dve.tensor_scalar(w_cl[:, c].bitcast(I32), w_pow[:, c].bitcast(I32), 0.0 if w in DVE_MEASURES else HALF, FLOOR,
                                  ALU.add, ALU.max).then_inc(w_cled, 1)
                dve.wait_ge(w_cled, w + 1)
                dve.tensor_scalar(w_scale[:, c].bitcast(I32), w_cl[:, c].bitcast(I32), -1.0, WTOP,
                                  ALU.mult, ALU.add).then_inc(w_scaled, 1)

            def w_low(w):
                dve.wait_ge(w_hi_done, w + 1)
                dve.wait_ge(w_scaled, w + 1)
                _, second, dst = w_src[w]
                hi, lo = parts(dst, second)
                dve.scalar_tensor_tensor(out=lo, in0=stage[w % STAGES], scalar=w_scale[:, w:w + 1], in1=hi,
                                         op0=ALU.mult, op1=ALU.subtract).then_inc(w_lo_done, 1)

            def w_low_half(w, i):
                dve.wait_ge((w_hi_half, w_hi_done)[i], w + 1)
                dve.wait_ge(w_scaled, w + 1)
                _, second, dst = w_src[w]
                hi, lo = parts(dst, second)
                dve.scalar_tensor_tensor(out=pieces(w, lo)[i], in0=pieces(w, stage[w % STAGES])[i],
                                         scalar=w_scale[:, w:w + 1], in1=pieces(w, hi)[i],
                                         op0=ALU.mult, op1=ALU.subtract).then_inc((w_lo_half, w_lo_done)[i], 1)

            def steps(s0, count, n, extra):
                for q in range(count):
                    h_low(s0 + q, q, n)
                    for fn in extra.get(q, ()):
                        fn()

            n_lab = [0]

            def lab_op(ins):
                n_lab[0] += 1
                ins.then_inc(lab_step, 1)
                dve.wait_ge(lab_step, n_lab[0])

            def labels_in():
                dve.wait_ge(lab_loaded, 16)
                dve.wait_ge(const_done, 7)
                lab_op(dve.tensor_copy(lab[:, 0:1], lab_i[:, :]))
                lab_op(dve.tensor_scalar(lab[:, 1:2], lab[:, 0:1], 0.0, float(NE), ALU.is_lt, ALU.mult))
                lab_op(dve.tensor_tensor(lab[:, 2:3], lab[:, 0:1], lab[:, 1:2], ALU.add))
                lab_op(dve.tensor_scalar(lab[:, 3:4], lab[:, 2:3], 0.0, float(NE - 1), ALU.max, ALU.min))
                lab_op(dve.tensor_scalar(onehot[:, :], label_no[:, :], lab[:, 3:4], None, ALU.is_equal))

            x_measure(0, 0, TG, 16, x_inv_early[:, 0, :])
            w_measure(0)
            x_low(0, 0, TG, lambda: w_scales(0))
            w_low_half(0, 0)
            w_measure(1)

            def place_slots():
                dve.wait_ge(lab_pe, 1)
                lab_op(dve.tensor_scalar(jobs_i[:, 0, :], tr[0][0:B, 0:NE], float(SLOTS - 1), None, ALU.add))
                lab_op(dve.tensor_scalar(jobs_i[:, 1, :], jobs_i[:, 0, :], 2, None, ALU.logical_shift_right))
                lab_op(dve.tensor_copy(jobs_f[:, 0, :], jobs_i[:, 1, :]))
                lab_op(dve.tensor_copy(cnt[:, 1, :], tr[0][0:B, 64:64 + NE]))
                lab_op(dve.tensor_tensor_scan(jobs_f[:, 1, :], ones[:, 0:NE], jobs_f[:, 0, :], 0.0, ALU.mult, ALU.add))
                lab_op(dve.tensor_tensor(jobs_f[:, 2, :], jobs_f[:, 1, :], jobs_f[:, 0, :], ALU.subtract))
                lab_op(dve.scalar_tensor_tensor(out=jobs_f[:, 3, :], in0=jobs_f[:, 2, :], scalar=float(SLOTS),
                                                in1=cnt[:, 1, :], op0=ALU.mult, op1=ALU.add))
                lab_op(dve.tensor_tensor(slot_of[:, 0:NE], jobs_f[:, 3, :], onehot[:, :], ALU.mult))
                lab_op(dve.tensor_reduce(slot_of[:, NE:NE + 1], slot_of[:, 0:NE], AX.X, ALU.add))
                lab_op(dve.tensor_scalar(slot_no2[:, :], slot_no[0:1, :], float(B), None, ALU.add))
                lab_op(dve.tensor_scalar(in_slot[:, :], slot_no[:, :], slot_of[:, NE:NE + 1], None, ALU.is_equal))

            slot_no2 = row0[:, 0, :]

            def name_slots():
                dve.wait_ge(lab_pe, 2)
                lab_op(dve.tensor_tensor(row0[:, 1, :], tr[0][0:1, 128:128 + NSLOT], slot_no2, ALU.mult))
                lab_op(dve.tensor_tensor(row0[:, 2, :], tr[0][0:1, 0:NSLOT], slot_no2, ALU.add))
                lab_op(dve.tensor_copy(slot_src[:, :], tr[0][0:1, 0:NSLOT]))
                lab_op(dve.tensor_tensor(row0[:, 3, :], row0[:, 2, :], row0[:, 1, :], ALU.subtract))
                lab_op(dve.tensor_copy(slot_dst[:, :], row0[:, 3, :]))
                lab_op(dve.tensor_tensor(cmp[:, :, :], job_no[:, :, :],
                                         jobs_f[0:1, 2:3, 1:NE].to_broadcast([1, JOBS, NE - 1]), ALU.is_ge))
                lab_op(dve.tensor_reduce(job_lab[:, :], cmp[:, :, :], AX.X, ALU.add))
                dve.tensor_copy(job_exp[:, :], job_lab[:, :]).then_inc(meta_done, 1)

            n_f = [0]

            def f_op(ins):
                n_f[0] += 1
                ins.then_inc(f_step, 1)
                dve.wait_ge(f_step, n_f[0])

            def f_measure():
                dve.wait_ge(f_loaded, 16)
                f_op(dve.tensor_reduce(f_max[:, :], f_nat[:, :], AX.X, ALU.max, apply_absolute_value=True))
                f_op(dve.tensor_scalar(f_pow[:, :].bitcast(I32), f_max[:, :].bitcast(I32), MASK, None, ALU.bitwise_and))
                f_op(dve.tensor_scalar(f_cl[:, :].bitcast(I32), f_pow[:, :].bitcast(I32), FLOOR, None, ALU.max))
                dve.tensor_scalar(f_scale[:, :].bitcast(I32), f_cl[:, :].bitcast(I32), -1.0, XTOP,
                                  ALU.mult, ALU.add).then_inc(f_scaled, 1)
                f_op(dve.tensor_scalar(f_inv[:, :], f_cl[:, :], 0.5, None, ALU.mult))

            def f_low():
                dve.wait_ge(f_hi_done, 1)
                dve.wait_ge(f_scaled, 1)
                dve.scalar_tensor_tensor(out=f_lo[:, :], in0=f_nat[:, :], scalar=f_scale[:, 0:1], in1=f_hi[:, :],
                                         op0=ALU.mult, op1=ALU.subtract).then_inc(f_lo_done, 1)

            def undo_scales():
                dve.wait_ge(w_cled, NW)
                f_op(dve.tensor_scalar(w_inv[:, :, :], w_cl[:, :].rearrange("p (n o) -> p n o", o=2), 1.0 / 16, None, ALU.mult))
                f_op(dve.tensor_tensor(pair_inv[:, :], w_inv[:, :, 0], w_inv[:, :, 1], ALU.mult))
                f_op(dve.tensor_tensor(lab_inv[:, 0:NE], onehot[:, :], pair_inv[0:B, NSH:NSH + NE], ALU.mult))
                f_op(dve.tensor_reduce(lab_inv[:, NE:NE + 1], lab_inv[:, 0:NE], AX.X, ALU.add))
                f_op(dve.tensor_scalar(f_fac[:, 0:1], lab_inv[:, NE:NE + 1], f_inv[:, 0:1], None, ALU.mult))
                f_op(dve.tensor_scalar(f_fac[:, 1:K3], pair_inv[0:B, 0:NSH], f_inv[:, 0:1], None, ALU.mult))
                f_op(dve.tensor_reduce(half_of[:, :], identf[0:B, 0:B].rearrange("b (g j) -> b j g", j=2), AX.X, ALU.add))
                f_op(dve.tensor_copy(half[:, :, :], half_of[:, :].rearrange("b (j o) -> b j o", o=1).to_broadcast([B, 2, S])))
                assert n_f[0] == F_FAC

            def load_expert(t, par, part):
                if part == 0:
                    if isinstance(t, int) and t < 2:
                        dve.wait_ge(w_lo_done, NW)
                    else:
                        dve.wait_ge(h_used, e_step(t - 1))
                e = dve.value_load(job_exp[0:1, bass.ds(t, 1)], min_val=0, max_val=NE - 1)
                src = w_exp[:, bass.ds(e, 1), part * WCOL:(part + 1) * WCOL].rearrange("p o n -> p (o n)")
                dve.tensor_copy(w_now[par][:, part * WCOL:(part + 1) * WCOL], src).then_inc(w_now_done, 1)

            extra = {q: [] for q in range(EARLY * SH)}
            extra[0] += [lambda: w_low_half(0, 1), lambda: w_scales(1)]
            extra[1] += [lambda: w_low_half(1, 0), lambda: w_low_half(1, 1)]
            for w in range(2, NW):
                if w in DVE_MEASURES:
                    extra[W_AT[w] - 1].append(lambda w=w: w_measure(w))
                extra[W_AT[w]].append(lambda w=w: w_scales(w))
                extra[W_AT[w] + 1].append(lambda w=w: w_low(w))
            extra[4].append(labels_in)
            extra[8].append(place_slots)
            extra[11].append(name_slots)
            extra[9].append(lambda: x_measure(1, 1, TG, 16, x_inv_early[:, 1, :]))
            extra[12].append(lambda: x_low(1, 1, TG))
            extra[14].append(f_measure)
            extra[17].append(f_low)
            extra[19].append(lambda: x_measure(e_x(0), 0, EG, 16 + 16 * SLOTS, None))
            extra[22].append(lambda: x_low(e_x(0), 0, EG))
            extra[31].append(undo_scales)
            steps(0, EARLY * SH, TOK, extra)
            steps(STEP_M, SH, B, {2 * i + 2: (lambda i=i: load_expert(0, 0, i),) for i in range(4)})

            def job(t, par, tail=None):
                nxt = t + 1
                ex = {}
                if tail is None:
                    cnt_ = 16 + 16 * SLOTS * ((nxt + 1) // 2 if par == 0 else nxt // 2 + 1)
                    ex[1] = [lambda: x_measure(e_x(nxt), 1 - par, EG, cnt_, None)]
                    ex[3] = [lambda: x_low(e_x(nxt), 1 - par, EG)]
                    for i, q in enumerate((3, 4, 5, 6)):
                        ex.setdefault(q, []).append(lambda i=i: load_expert(nxt, 1 - par, i))
                else:
                    ex = tail
                steps(e_step(t), FC, ETOK, ex)

            job(0, 0)
            with dve.Fori(0, (JOBS - 3) // 2) as pair:
                t = 2 * pair + 1
                job(t, 1)
                job(t + 1, 0)
            t = JOBS - 2
            job(t, 1)
            n = b_x(EARLY)
            xp = n % 2
            loads_e = {0: 16 + 16 * SLOTS * ((JOBS + 1) // 2), 1: 16 + 16 * SLOTS * (JOBS // 2)}

            def tile_loads(u, par):
                first = EARLY if par == xp else EARLY + 1
                return loads_e[par] + 16 * ((u - first) // 2 + 1)

            job(t + 1, 0, {1: (lambda: x_measure(n, xp, TG, tile_loads(EARLY, xp), x_inv[:, xp, :]),),
                           3: (lambda: x_low(n, xp, TG),)})

            n_g = [0]

            def g_op(ins):
                n_g[0] += 1
                ins.then_inc(gate_dve, 1)
                dve.wait_ge(gate_dve, n_g[0])

            def gate_rows():
                dve.wait_ge(ef_loaded, 16)
                g_op(dve.tensor_scalar(gate_in[:, 0, :], e_first, f_fac[:, 0:1], None, ALU.mult))
                g_op(dve.tensor_copy(pw[:, 0, 0:1], lab_inv[:, NE:NE + 1]))

            def gate_turned():
                dve.wait_ge(gate_pe, 1)
                g_op(dve.tensor_copy(gate_T.rearrange("p j b -> p (j b)"), tr[0][:, 0:K3 * DC * B]))

            def gate_relu():
                dve.wait_ge(gate_pe, 2)
                g_op(dve.tensor_scalar(gate_h.rearrange("p m b -> p (m b)"), tr[1][:, 0:DC * B], 0.0, None, ALU.max))

            def gate_max():
                dve.wait_ge(gate_pe, 3)
                g_op(dve.tensor_copy(logit[:, :], tr[0][0:B, 0:K3]))
                g_op(dve.tensor_reduce(lmax[:, :], logit[:, :], AX.X, ALU.max, negate=True))

            def gate_soft():
                dve.wait_ge(const_done, 8)
                dve.wait_ge(gate_act, 1)
                g_op(dve.tensor_reduce(psum_[:, :], prob[:, :], AX.X, ALU.add))
                g_op(dve.reciprocal(prec[:, :], psum_[:, :]))
                g_op(dve.tensor_copy(pw[:, 0, 1:K3], pair_inv[0:B, 0:NSH]))
                g_op(dve.scalar_tensor_tensor(out=pw[:, 1, :], in0=prob[:, :], scalar=prec[:, 0:1], in1=pw[:, 0, :],
                                              op0=ALU.mult, op1=ALU.mult))
                g_op(dve.tensor_tensor(spread[:, :, :],
                                       group[:, :].rearrange("b (g o) -> b g o", o=1).to_broadcast([B, GROUPS, K3]),
                                       pw[:, 1:2, :].to_broadcast([B, GROUPS, K3]), ALU.mult))

            def gate_out():
                dve.wait_ge(gate_pe, 4)
                g_op(dve.tensor_copy(w_tok[:, :, :].rearrange("p g k -> p (g k)"), tr[1][:, 0:GROUPS * K3]))

            def base(u, par, inv, n_en):
                dve.wait_ge(x_inv_done, u + 1)
                dve.tensor_tensor(fac[:, par], one_tile(u), inv, ALU.mult).then_inc(fac_done, 1)
                dve.wait_ge(fac_done, u - EARLY + 1)
                dve.wait_ge(en_loaded[par], n_en)
                xb = b_x(par) % 2
                for g in range(TG):
                    i = dve.scalar_tensor_tensor(out=acc[par][:, g, :], in0=e_nat[par][:, g, :], scalar=fac[:, par, g, 0:1],
                                                 in1=x_nat[:, xb, g, :], op0=ALU.mult, op1=ALU.add)
                i.then_inc(base_done, 1)

            def one_tile(u):
                return w_tok[:, TG * u:TG * (u + 1), :] if isinstance(u, int) else w_tok[:, bass.ds(TG * u, TG), :]

            def combine(u, par, k):
                dve.wait_ge(h_used, b_step(u) + (k + 1) * FC)
                if k == 0:
                    dve.wait_ge(base_done, u - EARLY + 1)
                else:
                    dve.wait_ge(combined, b_combined(u, 0))
                for g in range(TG):
                    i = dve.scalar_tensor_tensor(out=acc[par][:, g, :], in0=accb[2 * k + g // 2][:, (g % 2) * D:(g % 2 + 1) * D],
                                                 scalar=fac[:, par, g, 1 + k:2 + k], in1=acc[par][:, g, :],
                                                 op0=ALU.mult, op1=ALU.add)
                i.then_inc(combined, 1)

            def inv_of(par):
                xb = b_x(par) % 2
                return x_inv[:, xb, :].rearrange("p (g o) -> p g o", o=1).to_broadcast([P, TG, K3])

            def early_factors():
                dve.wait_ge(early_loaded, 32 * EARLY)
                for i in range(EARLY):
                    dve.tensor_tensor(fac_early[:, i], w_tok[:, TG * i:TG * (i + 1), :],
                                      x_inv_early[:, i, :].rearrange("p (g o) -> p g o", o=1).to_broadcast([P, TG, K3]),
                                      ALU.mult).then_inc(early_step, 1)
                dve.wait_ge(early_step, EARLY)

            def early_term(i, k):
                rows = e_early[i] if k == 0 else s_early[:, i, k - 1]
                for g in range(TG):
                    a = dve.scalar_tensor_tensor(out=x_early[i][:, g, :], in0=rows[:, g, :],
                                                 scalar=fac_early[:, i, g, k:k + 1],
                                                 in1=x_early[i][:, g, :], op0=ALU.mult, op1=ALU.add)
                a.then_inc(early_step, 1)
                dve.wait_ge(early_step, EARLY + K3 * i + k + 1)

            def tile(u, par, extra, n_next=None):
                m = {q: tuple(v) for q, v in extra.items()}
                if n_next is not None:
                    xb = b_x(par + 1) % 2
                    m[5] = m.get(5, ()) + (lambda: x_measure(b_x(u + 1), xb, TG, n_next, x_inv[:, xb, :]),)
                    m[7] = m.get(7, ()) + (lambda: x_low(b_x(u + 1), xb, TG),)
                steps(b_step(u), SH, TOK, m)

            def en_count(u, par):
                return 16 * ((u - par) // 2)

            def usual(u, par):
                return {2: (lambda: combine(u - 1, 1 - par, 1),), 3: (lambda: base(u, par, inv_of(par), en_count(u, par)),),
                        11: (lambda: combine(u, par, 0),)}

            tile(EARLY, 0, {6: (gate_rows,), 7: (gate_turned,), 8: (gate_relu,), 9: (gate_max,), 10: (gate_soft,),
                            12: (gate_out,),
                            13: (lambda: base(EARLY, 0, inv_of(0), 16),), 14: (lambda: combine(EARLY, 0, 0),)},
                 tile_loads(EARLY + 1, 1 - xp))
            with dve.Fori(0, (TILES - EARLY - 2) // 2) as pair:
                u = 2 * pair + EARLY + 1
                tile(u, 1, usual(u, 1), tile_loads(u + 1, xp))
                tile(u + 1, 0, usual(u + 1, 0), tile_loads(u + 2, 1 - xp))
            last = usual(TILES - 1, 1)
            last[4] = (early_factors,)
            for i in range(EARLY):
                for k in range(K3):
                    last.setdefault(5 + K3 * i + k, ())
                    last[5 + K3 * i + k] += (lambda i=i, k=k: early_term(i, k),)
            tile(TILES - 1, 1, last)
            combine(TILES - 1, 1, 1)


F_FAC = 12

W_AT = {2: 2, 3: 4, 4: 6, 5: 9, 6: 12, 7: 14, 8: 17, 9: 19, 10: 22, 11: 24, 12: 27, 13: 29}
DVE_MEASURES = (0, 1, 8, 10, 12)


def measured(w):
    return sum((v in DVE_MEASURES) == (w in DVE_MEASURES) for v in range(w + 1))


_INS = ['x', 'itok_B_0_2', 'L0_cond_wi', 'L0_cond_wo', 'L0_cond_swi', 'L0_cond_swo', 'L0_cond_g1', 'L0_cond_g2']


def kernel(**inputs):
    import numpy as _np
    import concourse.bacc as _bacc
    from concourse import mybir as _mybir
    from concourse.bass_utils import run_bass_kernel_spmd as _run

    nc = _bacc.Bacc("TRN2", target_bir_lowering=False, num_devices=1)
    arrays, args = {}, []
    for name in _INS:
        a = _np.ascontiguousarray(inputs[name])
        arrays[f"in_{name}_dram"] = a
        args.append(nc.dram_tensor(f"in_{name}_dram", a.shape, _mybir.dt.from_np(a.dtype), kind="ExternalInput").ap())
    shape = inputs['x'].shape
    args.append(nc.dram_tensor("out_0_dram", shape, _mybir.dt.float32, kind="ExternalOutput").ap())
    build(nc, *args)
    r = _run(nc, [arrays], core_ids=[0])
    return r.results[0]["out_0_dram"]
```

```python
from contextlib import ExitStack

import concourse.bass as bass
from concourse import mybir

F32 = mybir.dt.float32
F16 = mybir.dt.float16
I32 = mybir.dt.int32
ALU = mybir.AluOpType
ACT = mybir.ActivationFunctionType
AX = mybir.AxisListType
ABSMAX = bass.bass_isa.ReduceOp.absmax

P = 128



def build(nc, x, labels, wi, wo, swi, swo, g1, g2, out):
    B, S, D = x.shape
    NE, _, F = wi.shape
    NSH = swi.shape[0]
    DC = D // P
    FC = F // P
    TG = 4
    TOK = TG * P
    TILES = B * S // TOK
    SLOTS = 4
    EG = SLOTS * S // P
    ETOK = SLOTS * S
    QUADS = 12
    PAIRS = (B - SLOTS * QUADS + NE) // 2
    PTOK = 2 * S
    JOBS = QUADS + PAIRS
    QSLOTS = SLOTS * QUADS
    NSLOT = QSLOTS + 2 * PAIRS
    assert QSLOTS <= B - NE * (SLOTS - 1) + SLOTS - 1 and PAIRS == QUADS - 2 and PTOK == P
    GROUPS = B * S // P
    PERTILE = TOK // S
    K3 = 1 + NSH
    WCOL = DC * F
    assert WCOL == FC * D and S == 64 and TILES == 8 and B <= P

    LAG, RING, NP1 = 3, 4, 2
    SH = NSH * FC
    EARLY = 2
    STEP_M = EARLY * SH
    STEP_E = STEP_M + SH
    STEP_B = STEP_E + FC * JOBS

    def e_step(t):
        return STEP_E + FC * t

    def b_step(u):
        return STEP_B + SH * (u - EARLY)

    def quad(n):
        return n, SLOTS * n, SLOTS

    def pair(m):
        return QUADS + m, QSLOTS + 2 * m, 2

    def slots_before(t, par):
        return (SLOTS if par == 0 else 2) * ((t - par) // 2)

    def e_x(t):
        return EARLY + t

    def b_x(u):
        return JOBS + u

    def e_drained(t):
        return NSH * (EARLY + 1) + t + 1

    def b_combined(u, k):
        return NSH * (u - EARLY) + k + 1

    NW = 2 * NSH + 2 * NE
    STAGES = 4

    ctx = ExitStack()
    with ctx:
        def sb(name, shape, dt=F32):
            return ctx.enter_context(nc.sbuf_tensor(name, shape, dt))

        def sem(name):
            return ctx.enter_context(nc.semaphore(name))

        scratch = nc.dram_tensor("expert_rows", (B + NSLOT, S, D), F32, kind="Internal").ap()

        w_exp = sb("w_exp", [P, NE, 4 * WCOL], F16)
        w_sh = sb("w_sh", [P, NSH, 4 * WCOL], F16)
        region = sb("region", [P, 4 * WCOL], F32)
        stage = [region[:, s * WCOL:(s + 1) * WCOL] for s in range(STAGES)]
        w_now = [region[:, 2 * s * WCOL:2 * (s + 1) * WCOL].bitcast(F16) for s in range(2)]
        rg = region[:, :].rearrange("p (b g d) -> p b g d", g=TG, d=D)
        e_nat = [rg[:, i] for i in range(2)]
        acc = [rg[:, 2 + i] for i in range(2)]
        x_early = [rg[:, 4 + 2 * i] for i in range(EARLY)]
        e_early = [rg[:, 5 + 2 * i] for i in range(EARLY)]
        x_nat = sb("x_nat", [P, 2, TG, D])
        x_hi = sb("x_hi", [P, TG, D], F16)
        x_lo = sb("x_lo", [P, TG, D], F16)
        x_T = sb("x_T", [P, 2, 2, DC, TOK], F16)
        h_hi = sb("h_hi", [P, RING, TOK], F16)
        h_lo = sb("h_lo", [P, RING, TOK], F16)
        e_out = sb("e_out", [P, 2, EG, D])
        s_early = sb("s_early", [P, EARLY, NSH, TG, D])
        f_nat = sb("f_nat", [B, D])
        f_hi = sb("f_hi", [B, D], F16)
        f_lo = sb("f_lo", [B, D], F16)
        f_T = sb("f_T", [P, 2, DC, B], F16)
        x_max = sb("x_max", [P, TG]); x_pow = sb("x_pow", [P, TG]); x_cl = sb("x_cl", [P, TG])
        x_scale = sb("x_scale", [P, TG])
        x_inv = sb("x_inv", [P, 2, TG]); x_inv_early = sb("x_inv_early", [P, EARLY, TG])
        f_max = sb("f_max", [B, 1]); f_pow = sb("f_pow", [B, 1]); f_cl = sb("f_cl", [B, 1])
        f_scale = sb("f_scale", [B, 1]); f_inv = sb("f_inv", [B, 1])
        w_max = sb("w_max", [P, NW]); w_all = sb("w_all", [P, NW]); w_pow = sb("w_pow", [P, NW])
        w_cl = sb("w_cl", [P, NW])
        w_scale = sb("w_scale", [P, NW])
        w_inv = sb("w_inv", [P, NW // 2, 2])
        pair_inv = sb("pair_inv", [P, NW // 2])
        identf = sb("identf", [P, P]); ident = sb("ident", [P, P], F16)
        ones = sb("ones", [B, B])
        lower = sb("lower", [B, B])
        slot_no = sb("slot_no", [B, NSLOT])
        label_no = sb("label_no", [B, NE])
        job_no = sb("job_no", [1, QUADS, NE - 1])
        batch_no = sb("batch_no", [B, 1])
        half = sb("half", [B, 2, S])
        half_of = sb("half_of", [B, 2])
        group = sb("group", [B, GROUPS])
        lab_i = sb("lab_i", [B, 1], I32)
        lab = sb("lab", [B, 4])
        onehot = sb("onehot", [B, NE])
        jobs_i = sb("jobs_i", [B, 2, NE], I32)
        per_label = sb("per_label", [B, 18, NE])
        slot_of = sb("slot_of", [B, NE + 1])
        in_slot = sb("in_slot", [B, NSLOT])
        row0 = sb("row0", [1, 4, NSLOT])
        cmp = sb("cmp", [1, JOBS, NE - 1])
        job_lab = sb("job_lab", [1, JOBS])
        slot_src = sb("slot_src", [1, NSLOT], I32)
        slot_dst = sb("slot_dst", [1, NSLOT], I32)
        job_exp = sb("job_exp", [1, JOBS], I32)
        late = w_exp[:, 0].bitcast(F32)
        g1_sb = late[:, 0:K3 * DC * D].rearrange("p (j n) -> p j n", n=D)
        o = K3 * DC * D
        e_first = late[0:B, o:o + D]
        o += D
        gate_T = late[:, o:o + K3 * DC * B].rearrange("p (j b) -> p j b", b=B)
        o += K3 * DC * B
        gate_h = late[:, o:o + DC * B].rearrange("p (m b) -> p m b", b=B)
        g2_sb = sb("g2_sb", [P, DC, K3])
        gate_in = sb("gate_in", [B, K3, D])
        f_fac = sb("f_fac", [B, K3])
        lab_inv = sb("lab_inv", [B, NE + 1])
        logit = sb("logit", [B, K3]); lmax = sb("lmax", [B, 1])
        prob = sb("prob", [B, K3]); psum_ = sb("psum_", [B, 1]); prec = sb("prec", [B, 1])
        pw = sb("pw", [B, 3, K3])
        spread = sb("spread", [B, GROUPS, K3])
        w_tok = sb("w_tok", [P, GROUPS, K3])
        fac = sb("fac", [P, 2, TG, K3]); fac_early = sb("fac_early", [P, EARLY, TG, K3])

        def bank(name):
            return ctx.enter_context(nc.psum_tensor(name, [P, 512], F32))

        hid = [bank(f"hid{i}") for i in range(NP1)]
        accb = [bank(f"accb{i}") for i in range(4)]
        tr = [bank(f"tr{i}") for i in range(2)]

        x_loaded = [sem("x_loaded0"), sem("x_loaded1")]
        x_maxed, x_powed, x_cled, x_scaled = sem("x_maxed"), sem("x_powed"), sem("x_cled"), sem("x_scaled")
        x_hi_done, x_lo_done, x_turned, x_ready = sem("x_hi_done"), sem("x_lo_done"), sem("x_turned"), sem("x_ready")
        x_inv_done = sem("x_inv_done")
        f_loaded, f_step, f_scaled, f_hi_done, f_lo_done = sem("f_loaded"), sem("f_step"), sem("f_scaled"), sem("f_hi_done"), sem("f_lo_done")
        f_turned, f_ready = sem("f_turned"), sem("f_ready")
        w_loaded = [sem(f"w_loaded{i}") for i in range(STAGES)]
        w_maxed, w_reduced, w_powed, w_cled, w_scaled = sem("w_maxed"), sem("w_reduced"), sem("w_powed"), sem("w_cled"), sem("w_scaled")
        w_hi_done, w_lo_done, w_squared = sem("w_hi_done"), sem("w_lo_done"), sem("w_squared")
        w_hi_half, w_lo_half, x_hi_turned = sem("w_hi_half"), sem("w_lo_half"), sem("x_hi_turned")
        hid_full, h_hi_done, h_lo_done, h_used = sem("hid_full"), sem("h_hi_done"), sem("h_lo_done"), sem("h_used")
        acc_drained = sem("acc_drained")
        e_stored = [sem("e_stored0"), sem("e_stored1")]
        w_now_done = sem("w_now_done")
        const_step, const_done = sem("const_step"), sem("const_done")
        lab_loaded, lab_step, lab_pe, meta_done = sem("lab_loaded"), sem("lab_step"), sem("lab_pe"), sem("meta_done")
        g_loaded, ef_loaded = sem("g_loaded"), sem("ef_loaded")
        gate_dve, gate_pe, gate_act = sem("gate_dve"), sem("gate_pe"), sem("gate_act")
        early_loaded = sem("early_loaded")
        en_loaded = [sem("en_loaded0"), sem("en_loaded1")]
        fac_done, base_done, combined = sem("fac_done"), sem("base_done"), sem("combined")
        early_step, early_stored = sem("early_step"), sem("early_stored")
        stored = [sem("stored0"), sem("stored1")]

        block = ctx.enter_context(nc.Block())

        x_rows = x.rearrange("(t g h) s d -> t (h s) g d", g=TG, h=2)
        out_rows = out.rearrange("(t g h) s d -> t (h s) g d", g=TG, h=2)
        e_rows = scratch[0:B].rearrange("(t g h) s d -> t (h s) g d", g=TG, h=2)
        x_first = x[:, 0, :]
        e_first_rows = scratch[0:B, 0, :]

        w_src = []
        for k in range(NSH):
            w_src += [(swi[k], 0, w_sh[:, k]), (swo[k], 1, w_sh[:, k])]
        for k in range(NE):
            w_src += [(wi[k], 0, w_exp[:, k]), (wo[k], 1, w_exp[:, k])]

        def parts(w, second):
            o = 2 * WCOL * second
            return w[:, o:o + WCOL], w[:, o + WCOL:o + 2 * WCOL]

        def pieces(w, cols):
            v = cols.rearrange("p (c n) -> p c n", c=2)
            return (v[:, 0, :], v[:, 1, :]) if w_src[w][1] else (v[:, :, 0:F // 2], v[:, :, F // 2:F])

        @block.sync
        def _(sp):
            def need(s, v):
                if not isinstance(v, int) or v > 0:
                    sp.wait_ge(s, v)

            def load_weight(w):
                src, second, _ = w_src[w]
                if w >= STAGES:
                    sp.wait_ge(w_lo_done, w - STAGES + 1)
                v = src.rearrange("(c p) n -> p c n", p=P)
                dst = stage[w % STAGES].rearrange("p (c n) -> p c n", n=v.shape[2])
                sp.dma_start(dst, v).then_inc(w_loaded[w % STAGES], 16)

            def load_tile(u, n, par):
                need(x_lo_done, n - 1)
                sp.dma_start(x_nat[:, par], x_rows[u]).then_inc(x_loaded[par], 16)

            def load_slots(t, par, job):
                _, first, count = job
                need(x_lo_done, e_x(t) - 1)
                for j in range(count):
                    b = sp.value_load(slot_src[0:1, bass.ds(first + j, 1)], min_val=0, max_val=B - 1)
                    sp.dma_start(x_nat[S * (j % 2):S * (j % 2) + S, par, j // 2, :],
                                 x[bass.ds(b, 1)].rearrange("o s d -> (o s) d")).then_inc(x_loaded[par], 16)

            load_tile(0, 0, 0)
            load_weight(0)
            load_weight(1)
            load_weight(2)
            load_weight(3)
            sp.dma_start(lab_i[:, :], labels.rearrange("(b o) -> b o", o=1)).then_inc(lab_loaded, 16)
            load_tile(1, 1, 1)
            sp.dma_start(f_nat[:, :], x_first).then_inc(f_loaded, 16)
            sp.dma_start(g2_sb[:, :, :], g2.rearrange("(c p) n -> p c n", p=P)).then_inc(g_loaded, 16)
            for w in range(STAGES, 12):
                load_weight(w)
            sp.wait_ge(meta_done, 1)
            load_slots(0, 0, quad(0))
            load_weight(12)
            load_slots(1, 1, pair(0))
            load_weight(13)

            load_slots(2, 0, quad(1))
            with sp.Fori(0, PAIRS - 1) as i:
                t = 2 * i + 1
                load_slots(t + 2, 1, pair(i + 1))
                load_slots(t + 3, 0, quad(i + 2))
            load_slots(JOBS - 1, 1, quad(QUADS - 1))
            load_tile(EARLY, b_x(EARLY), b_x(EARLY) % 2)
            load_tile(EARLY + 1, b_x(EARLY + 1), b_x(EARLY + 1) % 2)
            sp.wait_ge(w_now_done, 4 * JOBS)
            sp.dma_start(g1_sb, g1.rearrange("(c p) n -> p c n", p=P)).then_inc(g_loaded, 16)
            sp.wait_ge(e_stored[0], 16 * SLOTS * (QUADS - 1))
            sp.wait_ge(e_stored[1], 16 * (2 * PAIRS + SLOTS))
            sp.dma_start(e_first, e_first_rows).then_inc(ef_loaded, 16)
            sp.wait_ge(h_used, STEP_B)
            for i in range(2):
                sp.dma_start(e_nat[i], e_rows[EARLY + i]).then_inc(en_loaded[i], 16)
            for i in range(EARLY):
                sp.dma_start(x_early[i], x_rows[i]).then_inc(early_loaded, 16)
                sp.dma_start(e_early[i], e_rows[i]).then_inc(early_loaded, 16)

            def store_tile(u):
                sp.wait_ge(combined, b_combined(u, NSH - 1))
                sp.dma_start(out_rows[u], acc[u % 2]).then_inc(stored[u % 2], 16)

            for u in range(EARLY, TILES):
                if u > EARLY:
                    store_tile(u - 1)
                    if u + 1 < TILES:
                        sp.wait_ge(stored[(u - 1) % 2], 16 * ((u - 1 - EARLY) // 2 + 1))
                        sp.dma_start(e_nat[(u + 1) % 2], e_rows[u + 1]).then_inc(en_loaded[(u + 1) % 2], 16)
                if u + 2 < TILES:
                    sp.wait_ge(base_done, u - EARLY + 1)
                    load_tile(u + 2, b_x(u + 2), b_x(u + 2) % 2)
            for i in range(EARLY):
                sp.wait_ge(early_step, EARLY + K3 * (i + 1))
                sp.dma_start(out_rows[i], x_early[i]).then_inc(early_stored, 16)
            store_tile(TILES - 1)
            sp.wait_ge(early_stored, 16 * EARLY)
            for i in range(2):
                sp.wait_ge(stored[i], 16 * (TILES - EARLY) // 2)

        @block.gpsimd
        def _(pool):
            n = [0]

            def ordered(ins):
                n[0] += 1
                ins.then_inc(const_step, 1)
                pool.wait_ge(const_step, n[0])

            ordered(pool.memset(identf[:, :], 0.0))
            pool.affine_select(out=identf[:, :], in_=identf[:, :], compare_op=ALU.not_equal, fill=1.0, base=0,
                               pattern=[[-1, P]], channel_multiplier=1).then_inc(const_done, 1)
            pool.wait_ge(const_done, 1)
            pool.tensor_copy(ident[:, :], identf[:, :]).then_inc(const_done, 1)

            def reduce_weight(w):
                if w in DVE_MEASURES:
                    pool.wait_ge(w_maxed, measured(w))
                else:
                    pool.wait_ge(w_squared, measured(w))
                pool.partition_all_reduce(w_all[:, w:w + 1], w_max[:, w:w + 1], P, ABSMAX).then_inc(w_reduced, 1)

            reduce_weight(0)
            ordered(pool.memset(ones[:, :], 1.0))
            pool.affine_select(out=lower[:, :], in_=ones[:, :], compare_op=ALU.is_gt, fill=0.0, base=0,
                               pattern=[[1, B]], channel_multiplier=-1).then_inc(const_done, 1)
            pool.iota(slot_no[:, :], [[1, NSLOT]], base=0, channel_multiplier=0,
                      allow_small_or_imprecise_dtypes=True).then_inc(const_done, 1)
            pool.iota(label_no[:, :], [[1, NE]], base=0, channel_multiplier=0,
                      allow_small_or_imprecise_dtypes=True).then_inc(const_done, 1)
            pool.iota(job_no[:, :, :], [[1, QUADS], [0, NE - 1]], base=0, channel_multiplier=0,
                      allow_small_or_imprecise_dtypes=True).then_inc(const_done, 1)
            pool.iota(batch_no[:, :], [[0, 1]], base=0, channel_multiplier=1,
                      allow_small_or_imprecise_dtypes=True).then_inc(const_done, 1)
            reduce_weight(1)
            ordered(pool.memset(group[:, :], 1.0))
            ordered(pool.affine_select(out=group[:, :], in_=group[:, :], compare_op=ALU.is_ge, fill=0.0, base=0,
                                       pattern=[[-2, GROUPS]], channel_multiplier=1))
            pool.affine_select(out=group[:, :], in_=group[:, :], compare_op=ALU.is_ge, fill=0.0, base=1,
                               pattern=[[2, GROUPS]], channel_multiplier=-1).then_inc(const_done, 1)
            for w in range(2, NW):
                reduce_weight(w)

            def store_slots(t, par, job):
                _, first, count = job
                pool.wait_ge(acc_drained, e_drained(t))
                for j in range(count):
                    r = pool.value_load(slot_dst[0:1, bass.ds(first + j, 1)], min_val=0, max_val=B + NSLOT - 1)
                    pool.dma_start(scratch[bass.ds(r, 1)].rearrange("o s d -> (o s) d"),
                                   e_out[S * (j % 2):S * (j % 2) + S, par, j // 2, :]).then_inc(e_stored[par], 16)

            pool.wait_ge(meta_done, 1)
            store_slots(0, 0, quad(0))
            with pool.Fori(0, PAIRS) as i:
                store_slots(2 * i + 1, 1, pair(i))
                store_slots(2 * i + 2, 0, quad(i + 1))
            store_slots(JOBS - 1, 1, quad(QUADS - 1))

        @block.tensor
        def _(pe):
            def need(s, v):
                if not isinstance(v, int) or v > 0:
                    pe.wait_ge(s, v)

            def hidden(s, f, w, rhs, n):
                need(h_lo_done, s - NP1 + 1)
                whi, wlo = parts(w, 0)
                for c in range(DC):
                    o = c * F + f * P
                    for i, (a, m) in enumerate(((whi, 0), (whi, 1), (wlo, 0))):
                        mm = pe.matmul(hid[f % NP1][:, 0:n], a[:, o:o + P], rhs(m, c),
                                       start=(c == 0 and i == 0), stop=(c == DC - 1 and i == 2))
                mm.then_inc(hid_full, 1)

            def project(s, f, w, groups, size, banks, wait=None, split=()):
                need(h_lo_done, s + 1)
                if f == 0 and wait is not None:
                    need(*wait)
                for which, count in split:
                    pe.wait_ge(which, count)
                whi, wlo = parts(w, 1)
                r = f % RING
                for g in range(groups):
                    o = accb[banks[g // 2]][0:size, (g % 2) * D:(g % 2) * D + D]
                    hh, hl = h_hi[:, r, g * P:g * P + size], h_lo[:, r, g * P:g * P + size]
                    for i, (a, b) in enumerate(((hh, whi), (hh, wlo), (hl, whi))):
                        mm = pe.matmul(o, a, b[:, f * D:f * D + D], start=(f == 0 and i == 0 and g % 2 == 0),
                                       stop=(f == FC - 1 and i == 2), skip_group_check=True)
                mm.then_inc(h_used, 1)

            def turn(n, groups, fixed=0):
                pe.wait_ge(x_lo_done, n + 1)
                need(x_ready, n)
                width = groups * P
                for m, src in enumerate((x_hi, x_lo)):
                    b = tr[m if groups == TG else 0][:, :].bitcast(F16)
                    o = 0 if groups == TG else m * DC * width
                    for c in range(DC):
                        for g in range(groups):
                            at = o + c * width + g * P
                            mm = pe.transpose(b[:, at:at + P], src[:, g, c * P:(c + 1) * P], ident[:, :])
                mm.then_inc(x_turned, 1)

            def tile_rhs(par, n):
                return lambda m, c: x_T[:, par, m, c, 0:n]

            class Tail:
                owed = []

            def step(s, f, w, rhs, n, proj):
                hidden(s, f, w, rhs, n)
                Tail.owed.append(proj)
                if len(Tail.owed) > LAG:
                    Tail.owed.pop(0)()

            def shared_steps(s0, par, waits, extra):
                for k in range(NSH):
                    for f in range(FC):
                        q = k * FC + f
                        for which, count in waits.get(("wi", q), ()):
                            pe.wait_ge(which, count)
                        step(s0 + q, f, w_sh[:, k], tile_rhs(par, TOK), TOK,
                             lambda q=q, k=k, f=f: project(s0 + q, f, w_sh[:, k], TG, P, (2 * k, 2 * k + 1),
                                                           waits.get(k), waits.get(("wo", q), ())))
                        for fn in extra.get(q, ()):
                            fn()

            def expert_steps(t, par, job, extra):
                tok = job[2] * S
                pe.wait_ge(x_ready, e_x(t) + 1)
                pe.wait_ge(w_now_done, 4 * t + 2)
                w = w_now[par]
                for f in range(FC):
                    step(e_step(t) + f, f, w, tile_rhs(par, tok), tok,
                         lambda f=f: project(e_step(t) + f, f, w, tok // P, P, (2 + par,), (acc_drained, e_drained(t) - 2),
                                             ((w_now_done, 4 * (t + 1)),) if f == 0 else ()))
                    for fn in extra.get(f, ()):
                        fn()

            pe.wait_ge(const_done, 2)
            for m, (src, there, seen) in enumerate(((x_hi, x_hi_done, x_hi_turned), (x_lo, x_lo_done, x_turned))):
                pe.wait_ge(there, 1)
                for c in range(DC):
                    for g in range(TG):
                        at = c * TOK + g * P
                        mm = pe.transpose(tr[m][:, :].bitcast(F16)[:, at:at + P], src[:, g, c * P:(c + 1) * P],
                                          ident[:, :])
                mm.then_inc(seen, 1)

            def count_labels():
                pe.wait_ge(const_done, 7)
                pe.wait_ge(lab_step, 5)
                pe.wait_ge(x_ready, 1)
                pe.matmul(tr[0][0:B, 0:NE], ones[:, :], onehot[:, :], start=True, stop=True)
                pe.matmul(tr[0][0:B, 64:64 + NE], lower[:, :], onehot[:, :], start=True, stop=True).then_inc(lab_pe, 1)

            def invert_slots():
                pe.wait_ge(lab_step, N_PLACED)
                pe.wait_ge(x_ready, 2)
                pe.matmul(tr[0][0:1, 0:NSLOT], batch_no[:, :], in_slot[:, :], start=True, stop=True)
                pe.matmul(tr[0][0:1, 128:128 + NSLOT], ones[:, 0:1], in_slot[:, :], start=True, stop=True).then_inc(lab_pe, 1)

            def turn_first():
                pe.wait_ge(f_lo_done, 1)
                pe.wait_ge(x_ready, 2)
                b = tr[1][:, :].bitcast(F16)
                for m, src in enumerate((f_hi, f_lo)):
                    for c in range(DC):
                        at = (m * DC + c) * B
                        mm = pe.transpose(b[:, at:at + B], src[:, c * P:(c + 1) * P], ident[0:B, 0:B])
                mm.then_inc(f_turned, 1)

            def turn_tile1():
                pe.wait_ge(lab_step, N_COUNTED)
                turn(1, TG)

            def turn_job0():
                pe.wait_ge(f_ready, 1)
                pe.wait_ge(meta_done, 1)
                turn(e_x(0), EG)

            pe.wait_ge(x_ready, 1)
            shared_steps(0, 0, {("wi", 0): ((w_lo_half, 1),), ("wi", FC // 2): ((w_lo_done, 1),),
                                ("wo", 0): ((w_lo_half, 2),), ("wo", FC // 2): ((w_lo_done, 2),),
                                ("wi", FC): ((w_lo_done, 3),), ("wo", FC): ((w_lo_done, 4),)},
                         {5: (count_labels,), 12: (turn_tile1,)})
            pe.wait_ge(x_ready, 2)
            shared_steps(SH, 1, {0: (acc_drained, 1), 1: (acc_drained, 2)}, {0: (invert_slots,), 5: (turn_first,), 13: (turn_job0,)})

            pe.wait_ge(f_ready, 1)
            for k in range(NSH):
                for f in range(FC):
                    q = STEP_M + k * FC + f
                    step(q, f, w_sh[:, k], lambda m, c: f_T[:, m, c, :], B,
                         lambda q=q, k=k, f=f: project(q, f, w_sh[:, k], 1, B, (k,), (acc_drained, NSH + 1)))

            def four_steps(t, n, after):
                expert_steps(t, 0, quad(n), {3: (lambda: turn(e_x(t + 1), after[2] * S // P),)})

            def pair_steps(t, m):
                expert_steps(t, 1, pair(m), {1: (lambda: turn(e_x(t + 1), EG),)})

            def owed_quad(t):
                return [lambda q=q: project(e_step(t) + q, q, w_now[0], EG, P, (2,)) for q in range(FC - LAG, FC)]

            four_steps(0, 0, pair(0))
            with pe.Fori(0, PAIRS - 1) as i:
                t = 2 * i + 1
                Tail.owed = owed_quad(t - 1)
                pair_steps(t, i)
                four_steps(t + 1, i + 1, pair(i + 1))
            t = JOBS - 3
            Tail.owed = owed_quad(t - 1)
            pair_steps(t, PAIRS - 1)
            four_steps(t + 1, QUADS - 2, quad(QUADS - 1))
            expert_steps(t + 2, 1, quad(QUADS - 1), {5: (lambda: turn(b_x(EARLY), TG),)})

            def turn_gate():
                pe.wait_ge(gate_dve, 2)
                pe.wait_ge(acc_drained, NSH * (EARLY + 1))
                pe.wait_ge(x_ready, b_x(EARLY) + 1)
                for j in range(K3 * DC):
                    mm = pe.transpose(tr[0][:, j * B:(j + 1) * B],
                                      gate_in[:, j // DC, (j % DC) * P:(j % DC + 1) * P], identf[0:B, 0:B])
                mm.then_inc(gate_pe, 1)

            def gate_hidden():
                pe.wait_ge(gate_dve, 3)
                pe.wait_ge(g_loaded, 32)
                for m in range(DC):
                    for j in range(K3 * DC):
                        mm = pe.matmul(tr[1][:, m * B:(m + 1) * B], g1_sb[:, j, m * P:(m + 1) * P], gate_T[:, j, :],
                                       start=(j == 0), stop=(j == K3 * DC - 1))
                mm.then_inc(gate_pe, 1)

            def gate_logits():
                pe.wait_ge(gate_dve, 4)
                for m in range(DC):
                    mm = pe.matmul(tr[0][0:B, 0:K3], gate_h[:, m, :], g2_sb[:, m, :], start=(m == 0), stop=(m == DC - 1))
                mm.then_inc(gate_pe, 1)

            def gate_tokens():
                pe.wait_ge(gate_dve, 11)
                pe.matmul(tr[1][:, 0:GROUPS * K3], half[:, :, :].rearrange("b h s -> b (h s)"),
                          spread[:, :, :].rearrange("b g k -> b (g k)"), start=True, stop=True).then_inc(gate_pe, 1)

            def tile_steps(u, par, extra):
                pe.wait_ge(x_ready, b_x(u) + 1)
                first = isinstance(u, int) and u == EARLY
                waits = {0: (acc_drained, NSH * (EARLY + 1)), 1: (acc_drained, e_drained(JOBS - 1))} if first else {
                    k: (combined, b_combined(u - 1, k)) for k in range(NSH)}
                shared_steps(b_step(u), par, waits, extra)

            def next_tile(u):
                return {10: (lambda: turn(b_x(u + 1), TG),)}

            def owed_shared(s0):
                return [lambda q=q: project(s0 + q, q % FC, w_sh[:, NSH - 1], TG, P, (2, 3)) for q in range(SH - LAG, SH)]

            xp = b_x(EARLY) % 2
            tile_steps(EARLY, xp, {6: (turn_gate,), 7: (gate_hidden,), 8: (gate_logits,), 11: (gate_tokens,),
                                   13: (lambda: (pe.wait_ge(gate_dve, 12), turn(b_x(EARLY + 1), TG)),)})
            with pe.Fori(0, (TILES - EARLY - 2) // 2) as i:
                u = 2 * i + EARLY + 1
                Tail.owed = owed_shared(b_step(u - 1))
                tile_steps(u, 1 - xp, next_tile(u))
                tile_steps(u + 1, xp, next_tile(u + 1))
            Tail.owed = owed_shared(b_step(TILES - 2))
            tile_steps(TILES - 1, 1 - xp, {})
            while Tail.owed:
                Tail.owed.pop(0)()

        @block.scalar
        def _(act):
            def need(s, v):
                if not isinstance(v, int) or v > 0:
                    act.wait_ge(s, v)

            def relu_hi(s, f, n):
                act.wait_ge(hid_full, s + 1)
                need(h_used, s - RING + 1)
                act.activation(h_hi[:, f % RING, 0:n], hid[f % NP1][:, 0:n], ACT.Relu).then_inc(h_hi_done, 1)

            def x_split(n, par, groups):
                act.wait_ge(x_scaled, n + 1)
                need(x_turned, n)
                for g in range(groups):
                    a = act.activation(x_hi[:, g, :], x_nat[:, par, g, :], ACT.Copy, scale=x_scale[:, g:g + 1])
                a.then_inc(x_hi_done, 1)

            def x_keep(n, par, groups):
                act.wait_ge(x_turned, n + 1)
                if groups == TG:
                    for m in range(2):
                        a = act.activation(x_T[:, par, m, :, :], tr[m][:, :].bitcast(F16).rearrange("p (c t) -> p c t", c=DC),
                                           ACT.Copy)
                else:
                    a = act.activation(x_T[:, par, :, :, 0:groups * P],
                                       tr[0][:, :].bitcast(F16)[:, 0:2 * DC * groups * P]
                                       .rearrange("p (m c t) -> p m c t", m=2, c=DC), ACT.Copy)
                a.then_inc(x_ready, 1)

            def w_split(w):
                act.wait_ge(w_scaled, w + 1)
                _, second, dst = w_src[w]
                act.activation(parts(dst, second)[0], stage[w % STAGES], ACT.Copy,
                               scale=w_scale[:, w:w + 1]).then_inc(w_hi_done, 1)

            def w_split_half(w, i):
                if i == 0:
                    act.wait_ge(w_scaled, w + 1)
                _, second, dst = w_src[w]
                act.activation(pieces(w, parts(dst, second)[0])[i], pieces(w, stage[w % STAGES])[i], ACT.Copy,
                               scale=w_scale[:, w:w + 1]).then_inc((w_hi_half, w_hi_done)[i], 1)

            def w_square(w):
                act.wait_ge(w_loaded[w % STAGES], 16 * (w // STAGES + 1))
                _, second, dst = w_src[w]
                act.activation(parts(dst, second)[1], stage[w % STAGES], ACT.Square,
                               accum_out=w_max[:, w:w + 1]).then_inc(w_squared, 1)

            def steps(s0, count, n, extra):
                for q in range(count):
                    relu_hi(s0 + q, q, n)
                    for fn in extra.get(q, ()):
                        fn()

            x_split(0, 0, TG)
            for m, seen in enumerate((x_hi_turned, x_turned)):
                if m == 1:
                    w_split_half(0, 0)
                act.wait_ge(seen, 1)
                a = act.activation(x_T[:, 0, m, :, :], tr[m][:, :].bitcast(F16).rearrange("p (c t) -> p c t", c=DC),
                                   ACT.Copy)
            a.then_inc(x_ready, 1)
            w_split_half(0, 1)

            def drain_early(i, k):
                act.wait_ge(h_used, i * SH + (k + 1) * FC)
                for h in range(2):
                    a = act.activation(s_early[:, i, k, 2 * h:2 * h + 2, :],
                                       accb[2 * k + h][:, :].rearrange("p (g d) -> p g d", d=D), ACT.Copy)
                a.then_inc(acc_drained, 1)

            def f_split():
                act.wait_ge(f_scaled, 1)
                act.activation(f_hi[:, :], f_nat[:, :], ACT.Copy, scale=f_scale[:, 0:1]).then_inc(f_hi_done, 1)

            def f_keep():
                act.wait_ge(f_turned, 1)
                act.activation(f_T[:, :, :, :].rearrange("p m c b -> p (m c b)"),
                               tr[1][:, :].bitcast(F16)[:, 0:2 * DC * B], ACT.Copy).then_inc(f_ready, 1)

            extra = {q: [] for q in range(EARLY * SH)}
            extra[0].append(lambda: w_split_half(1, 0))
            extra[1].append(lambda: w_split_half(1, 1))
            extra[9].append(lambda: x_split(1, 1, TG))
            extra[14].append(lambda: x_keep(1, 1, TG))
            for w in range(2, NW):
                if w not in DVE_MEASURES:
                    extra[W_AT[w] - 1].append(lambda w=w: w_square(w))
                extra[W_AT[w]].append(lambda w=w: w_split(w))
            extra[19].append(f_split)
            extra[16].append(lambda: drain_early(0, 0))
            extra[22].append(lambda: drain_early(0, 1))
            extra[23].append(f_keep)
            extra[26].append(lambda: x_split(e_x(0), 0, EG))
            extra[27].append(lambda: drain_early(1, 0))
            extra[31].append(lambda: x_keep(e_x(0), 0, EG))
            steps(0, EARLY * SH, TOK, extra)

            def drain_first(k):
                act.wait_ge(h_used, STEP_M + (k + 1) * FC)
                act.wait_ge(f_step, F_FAC)
                act.activation(gate_in[:, 1 + k, :], accb[k][0:B, 0:D], ACT.Copy,
                               scale=f_fac[:, 1 + k:2 + k]).then_inc(acc_drained, 1)

            steps(STEP_M, SH, B, {2: (lambda: drain_early(1, 1),), FC + 3: (lambda: drain_first(0),)})

            def drain_job(t, par, job):
                act.wait_ge(h_used, e_step(t + 1))
                if not isinstance(t, int) or t >= 2:
                    act.wait_ge(e_stored[par], 16 * slots_before(t, par))
                groups = job[2] * S // P
                act.activation(e_out[:, par, 0:groups].rearrange("p g d -> p (g d)"), accb[2 + par][:, 0:groups * D],
                               ACT.Copy).then_inc(acc_drained, 1)

            def four_job(t, ended):
                ex = {1: (lambda: x_split(e_x(t + 1), 1, PTOK // P),), 4: (lambda: x_keep(e_x(t + 1), 1, PTOK // P),),
                      5: (lambda: x_split(e_x(t + 2), 0, EG),)}
                steps(e_step(t), FC, ETOK, {2: (lambda: drain_job(t - 1, 1, ended) if ended else drain_first(1),), **ex})

            def pair_job(t, ended):
                steps(e_step(t), FC, PTOK, {2: (lambda: drain_job(t - 1, 0, ended),), 3: (lambda: x_keep(e_x(t + 1), 0, EG),)})

            four_job(0, None)
            pair_job(1, quad(0))
            four_job(2, pair(0))
            with act.Fori(0, PAIRS - 2) as i:
                t = 2 * i + 3
                pair_job(t, quad(i + 1))
                four_job(t + 1, pair(i + 1))
            t = JOBS - 3
            pair_job(t, quad(QUADS - 3))
            steps(e_step(t + 1), FC, ETOK, {1: (lambda: x_split(e_x(t + 2), 1, EG),),
                                            2: (lambda: drain_job(t, 1, pair(PAIRS - 1)),),
                                            4: (lambda: x_keep(e_x(t + 2), 1, EG),)})
            n = b_x(EARLY)
            steps(e_step(t + 2), FC, ETOK, {2: (lambda: drain_job(t + 1, 0, quad(QUADS - 2)),),
                                            3: (lambda: x_split(n, n % 2, TG),), 6: (lambda: x_keep(n, n % 2, TG),)})

            def softmax_exp():
                act.wait_ge(gate_dve, 6)
                act.activation(prob[:, :], logit[:, :], ACT.Exp, bias=lmax[:, 0:1]).then_inc(gate_act, 1)

            def tile(u, par, extra, more=True):
                m = dict(extra)
                if more:
                    n = b_x(u + 1)
                    m.setdefault(6, ()); m.setdefault(11, ())
                    at_keep = 14 if isinstance(u, int) else 11
                    m[6] = m[6] + (lambda: x_split(n, par, TG),)
                    m[at_keep] = m.get(at_keep, ()) + (lambda: x_keep(n, par, TG),)
                steps(b_step(u), SH, TOK, m)

            xp = b_x(EARLY) % 2
            tile(EARLY, 1 - xp, {2: (lambda: drain_job(JOBS - 1, 1, quad(QUADS - 1)),), 10: (softmax_exp,)})
            with act.Fori(0, (TILES - EARLY - 2) // 2) as i:
                u = 2 * i + EARLY + 1
                tile(u, xp, {})
                tile(u + 1, 1 - xp, {})
            tile(TILES - 1, xp, {}, more=False)

        @block.vector
        def _(dve):
            def need(s, v):
                if not isinstance(v, int) or v > 0:
                    dve.wait_ge(s, v)

            MASK = 0x7F800000
            FLOOR = float(77 << 23)
            XTOP = float(255 << 23)
            WTOP = float(258 << 23)
            HALF = float(64 << 23)

            def h_low(s, f, n):
                dve.wait_ge(h_hi_done, s + 1)
                dve.scalar_tensor_tensor(out=h_lo[:, f % RING, 0:n], in0=hid[f % NP1][:, 0:n], scalar=0.0,
                                         in1=h_hi[:, f % RING, 0:n], op0=ALU.max, op1=ALU.subtract).then_inc(h_lo_done, 1)

            def x_measure(n, par, groups, loads, inv):
                dve.wait_ge(x_loaded[par], loads)
                dve.tensor_reduce(x_max[:, 0:groups], x_nat[:, par, 0:groups, :], AX.X, ALU.max,
                                  apply_absolute_value=True).then_inc(x_maxed, 1)
                dve.wait_ge(x_maxed, n + 1)
                dve.tensor_scalar(x_pow[:, 0:groups].bitcast(I32), x_max[:, 0:groups].bitcast(I32), MASK, None,
                                  ALU.bitwise_and).then_inc(x_powed, 1)
                dve.wait_ge(x_powed, n + 1)
                dve.tensor_scalar(x_cl[:, 0:groups].bitcast(I32), x_pow[:, 0:groups].bitcast(I32), FLOOR, None,
                                  ALU.max).then_inc(x_cled, 1)
                dve.wait_ge(x_cled, n + 1)
                dve.tensor_scalar(x_scale[:, 0:groups].bitcast(I32), x_cl[:, 0:groups].bitcast(I32), -1.0, XTOP,
                                  ALU.mult, ALU.add).then_inc(x_scaled, 1)
                if inv is not None:
                    dve.tensor_scalar(inv, x_cl[:, :], 0.5, None, ALU.mult).then_inc(x_inv_done, 1)

            def x_low(n, par, groups, between=None):
                dve.wait_ge(x_hi_done, n + 1)
                for g in range(groups):
                    if between is not None and g == 3:
                        between()
                    i = dve.scalar_tensor_tensor(out=x_lo[:, g, :], in0=x_nat[:, par, g, :], scalar=x_scale[:, g:g + 1],
                                                 in1=x_hi[:, g, :], op0=ALU.mult, op1=ALU.subtract)
                i.then_inc(x_lo_done, 1)

            def w_measure(w):
                dve.wait_ge(w_loaded[w % STAGES], 16 * (w // STAGES + 1))
                dve.tensor_reduce(w_max[:, w:w + 1], stage[w % STAGES], AX.X, ALU.max,
                                  apply_absolute_value=True).then_inc(w_maxed, 1)

            def w_scales(w):
                dve.wait_ge(w_reduced, w + 1)
                c = slice(w, w + 1)
                if w not in DVE_MEASURES:
                    dve.tensor_scalar(w_pow[:, c].bitcast(I32), w_all[:, c].bitcast(I32), 1, MASK,
                                      ALU.logical_shift_right, ALU.bitwise_and).then_inc(w_powed, 1)
                else:
                    dve.tensor_scalar(w_pow[:, c].bitcast(I32), w_all[:, c].bitcast(I32), MASK, None,
                                      ALU.bitwise_and).then_inc(w_powed, 1)
                dve.wait_ge(w_powed, w + 1)
                dve.tensor_scalar(w_cl[:, c].bitcast(I32), w_pow[:, c].bitcast(I32), 0.0 if w in DVE_MEASURES else HALF, FLOOR,
                                  ALU.add, ALU.max).then_inc(w_cled, 1)
                dve.wait_ge(w_cled, w + 1)
                dve.tensor_scalar(w_scale[:, c].bitcast(I32), w_cl[:, c].bitcast(I32), -1.0, WTOP,
                                  ALU.mult, ALU.add).then_inc(w_scaled, 1)

            def w_low(w):
                dve.wait_ge(w_hi_done, w + 1)
                dve.wait_ge(w_scaled, w + 1)
                _, second, dst = w_src[w]
                hi, lo = parts(dst, second)
                dve.scalar_tensor_tensor(out=lo, in0=stage[w % STAGES], scalar=w_scale[:, w:w + 1], in1=hi,
                                         op0=ALU.mult, op1=ALU.subtract).then_inc(w_lo_done, 1)

            def w_low_half(w, i):
                dve.wait_ge((w_hi_half, w_hi_done)[i], w + 1)
                dve.wait_ge(w_scaled, w + 1)
                _, second, dst = w_src[w]
                hi, lo = parts(dst, second)
                dve.scalar_tensor_tensor(out=pieces(w, lo)[i], in0=pieces(w, stage[w % STAGES])[i],
                                         scalar=w_scale[:, w:w + 1], in1=pieces(w, hi)[i],
                                         op0=ALU.mult, op1=ALU.subtract).then_inc((w_lo_half, w_lo_done)[i], 1)

            def steps(s0, count, n, extra):
                for q in range(count):
                    h_low(s0 + q, q, n)
                    for fn in extra.get(q, ()):
                        fn()

            n_lab = [0]

            def lab_op(ins):
                n_lab[0] += 1
                ins.then_inc(lab_step, 1)
                dve.wait_ge(lab_step, n_lab[0])

            def labels_in():
                dve.wait_ge(lab_loaded, 16)
                dve.wait_ge(const_done, 7)
                lab_op(dve.tensor_copy(lab[:, 0:1], lab_i[:, :]))
                lab_op(dve.tensor_scalar(lab[:, 1:2], lab[:, 0:1], 0.0, float(NE), ALU.is_lt, ALU.mult))
                lab_op(dve.tensor_tensor(lab[:, 2:3], lab[:, 0:1], lab[:, 1:2], ALU.add))
                lab_op(dve.tensor_scalar(lab[:, 3:4], lab[:, 2:3], 0.0, float(NE - 1), ALU.max, ALU.min))
                lab_op(dve.tensor_scalar(onehot[:, :], label_no[:, :], lab[:, 3:4], None, ALU.is_equal))

            x_measure(0, 0, TG, 16, x_inv_early[:, 0, :])
            w_measure(0)
            x_low(0, 0, TG, lambda: w_scales(0))
            w_low_half(0, 0)
            w_measure(1)
            w_scales(1)

            count, rank, whole, four_to, four_before, four_taken, in_four, left, pairs, pairs_to, pairs_before = (
                per_label[:, i, :] for i in range(11))
            place_four, place_pair, apart, apart2, is_left, move, place = (per_label[:, 11 + i, :] for i in range(7))

            def count_fours():
                dve.wait_ge(lab_pe, 1)
                lab_op(dve.tensor_scalar(jobs_i[:, 0, :], tr[0][0:B, 0:NE], 0.0, None, ALU.add))
                lab_op(dve.tensor_copy(count, tr[0][0:B, 0:NE]))
                lab_op(dve.tensor_copy(rank, tr[0][0:B, 64:64 + NE]))
                assert n_lab[0] == N_COUNTED
                lab_op(dve.tensor_scalar(jobs_i[:, 1, :], jobs_i[:, 0, :], 2, None, ALU.logical_shift_right))
                lab_op(dve.tensor_copy(whole, jobs_i[:, 1, :]))
                lab_op(dve.tensor_tensor_scan(four_to, ones[:, 0:NE], whole, 0.0, ALU.mult, ALU.add))
                lab_op(dve.tensor_tensor(four_before, four_to, whole, ALU.subtract))
                lab_op(dve.tensor_scalar(per_label[:, 3:5, :], per_label[:, 3:5, :], float(QUADS), None, ALU.min))
                lab_op(dve.tensor_tensor(four_taken, four_to, four_before, ALU.subtract))

            def count_pairs():
                lab_op(dve.tensor_scalar(in_four, four_taken, float(SLOTS), None, ALU.mult))
                lab_op(dve.tensor_tensor(left, count, in_four, ALU.subtract))
                lab_op(dve.tensor_scalar(jobs_i[:, 0, :], left, 1.0, None, ALU.add))
                lab_op(dve.tensor_scalar(jobs_i[:, 1, :], jobs_i[:, 0, :], 1, None, ALU.logical_shift_right))
                lab_op(dve.tensor_copy(pairs, jobs_i[:, 1, :]))
                lab_op(dve.tensor_tensor_scan(pairs_to, ones[:, 0:NE], pairs, 0.0, ALU.mult, ALU.add))
                lab_op(dve.tensor_tensor(pairs_before, pairs_to, pairs, ALU.subtract))

            def place_slots():
                lab_op(dve.scalar_tensor_tensor(out=place_four, in0=four_before, scalar=float(SLOTS), in1=rank,
                                                op0=ALU.mult, op1=ALU.add))
                lab_op(dve.scalar_tensor_tensor(out=place_pair, in0=pairs_before, scalar=2.0, in1=rank,
                                                op0=ALU.mult, op1=ALU.add))
                lab_op(dve.tensor_tensor(apart, place_pair, place_four, ALU.subtract))
                lab_op(dve.tensor_tensor(apart2, apart, in_four, ALU.subtract))
                lab_op(dve.tensor_tensor(is_left, rank, in_four, ALU.is_ge))

            def fill_slots():
                lab_op(dve.scalar_tensor_tensor(out=move, in0=apart2, scalar=float(QSLOTS), in1=is_left,
                                                op0=ALU.add, op1=ALU.mult))
                lab_op(dve.tensor_tensor(place, place_four, move, ALU.add))
                lab_op(dve.tensor_tensor(slot_of[:, 0:NE], place, onehot[:, :], ALU.mult))
                lab_op(dve.tensor_reduce(slot_of[:, NE:NE + 1], slot_of[:, 0:NE], AX.X, ALU.add))
                lab_op(dve.tensor_scalar(slot_no2, slot_no[0:1, :], float(B), None, ALU.add))
                lab_op(dve.tensor_scalar(in_slot[:, :], slot_no[:, :], slot_of[:, NE:NE + 1], None, ALU.is_equal))
                assert n_lab[0] == N_PLACED

            slot_no2 = row0[:, 0, :]

            def name_slots():
                dve.wait_ge(lab_pe, 2)
                lab_op(dve.tensor_tensor(row0[:, 1, :], tr[0][0:1, 128:128 + NSLOT], slot_no2, ALU.mult))
                lab_op(dve.tensor_tensor(row0[:, 2, :], tr[0][0:1, 0:NSLOT], slot_no2, ALU.add))
                lab_op(dve.tensor_copy(slot_src[:, :], tr[0][0:1, 0:NSLOT]))
                lab_op(dve.tensor_tensor(row0[:, 3, :], row0[:, 2, :], row0[:, 1, :], ALU.subtract))
                lab_op(dve.tensor_copy(slot_dst[:, :], row0[:, 3, :]))
                lab_op(dve.tensor_tensor(cmp[:, 0:QUADS, :], job_no[:, 0:QUADS, :],
                                         per_label[0:1, 4:5, 1:NE].to_broadcast([1, QUADS, NE - 1]), ALU.is_ge))
                lab_op(dve.tensor_tensor(cmp[:, QUADS:JOBS, :], job_no[:, 0:PAIRS, :],
                                         per_label[0:1, 10:11, 1:NE].to_broadcast([1, PAIRS, NE - 1]), ALU.is_ge))
                lab_op(dve.tensor_reduce(job_lab[:, :], cmp[:, :, :], AX.X, ALU.add))
                dve.tensor_copy(job_exp[:, :], job_lab[:, :]).then_inc(meta_done, 1)

            n_f = [0]

            def f_op(ins):
                n_f[0] += 1
                ins.then_inc(f_step, 1)
                dve.wait_ge(f_step, n_f[0])

            def f_measure():
                dve.wait_ge(f_loaded, 16)
                f_op(dve.tensor_reduce(f_max[:, :], f_nat[:, :], AX.X, ALU.max, apply_absolute_value=True))
                f_op(dve.tensor_scalar(f_pow[:, :].bitcast(I32), f_max[:, :].bitcast(I32), MASK, None, ALU.bitwise_and))
                f_op(dve.tensor_scalar(f_cl[:, :].bitcast(I32), f_pow[:, :].bitcast(I32), FLOOR, None, ALU.max))
                dve.tensor_scalar(f_scale[:, :].bitcast(I32), f_cl[:, :].bitcast(I32), -1.0, XTOP,
                                  ALU.mult, ALU.add).then_inc(f_scaled, 1)
                f_op(dve.tensor_scalar(f_inv[:, :], f_cl[:, :], 0.5, None, ALU.mult))

            def f_low():
                dve.wait_ge(f_hi_done, 1)
                dve.wait_ge(f_scaled, 1)
                dve.scalar_tensor_tensor(out=f_lo[:, :], in0=f_nat[:, :], scalar=f_scale[:, 0:1], in1=f_hi[:, :],
                                         op0=ALU.mult, op1=ALU.subtract).then_inc(f_lo_done, 1)

            def undo_scales():
                dve.wait_ge(w_cled, NW)
                f_op(dve.tensor_scalar(w_inv[:, :, :], w_cl[:, :].rearrange("p (n o) -> p n o", o=2), 1.0 / 16, None, ALU.mult))
                f_op(dve.tensor_tensor(pair_inv[:, :], w_inv[:, :, 0], w_inv[:, :, 1], ALU.mult))
                f_op(dve.tensor_tensor(lab_inv[:, 0:NE], onehot[:, :], pair_inv[0:B, NSH:NSH + NE], ALU.mult))
                f_op(dve.tensor_reduce(lab_inv[:, NE:NE + 1], lab_inv[:, 0:NE], AX.X, ALU.add))
                f_op(dve.tensor_scalar(f_fac[:, 0:1], lab_inv[:, NE:NE + 1], f_inv[:, 0:1], None, ALU.mult))
                f_op(dve.tensor_scalar(f_fac[:, 1:K3], pair_inv[0:B, 0:NSH], f_inv[:, 0:1], None, ALU.mult))
                f_op(dve.tensor_reduce(half_of[:, :], identf[0:B, 0:B].rearrange("b (g j) -> b j g", j=2), AX.X, ALU.add))
                f_op(dve.tensor_copy(half[:, :, :], half_of[:, :].rearrange("b (j o) -> b j o", o=1).to_broadcast([B, 2, S])))
                assert n_f[0] == F_FAC

            expert = [None, None]

            def look_up(par, job):
                expert[par] = dve.value_load(job_exp[0:1, bass.ds(job[0], 1)], min_val=0, max_val=NE - 1)

            def load_expert(t, par, job, part):
                if isinstance(t, int) and t < 2:
                    if part == 0:
                        dve.wait_ge(w_lo_done, NW)
                elif part == 0:
                    dve.wait_ge(hid_full, e_step(t - 1))
                elif part == 2:
                    dve.wait_ge(h_used, e_step(t - 1))
                src = w_exp[:, bass.ds(expert[par], 1), part * WCOL:(part + 1) * WCOL].rearrange("p o n -> p (o n)")
                dve.tensor_copy(w_now[par][:, part * WCOL:(part + 1) * WCOL], src).then_inc(w_now_done, 1)

            extra = {q: [] for q in range(EARLY * SH)}
            extra[0].append(lambda: w_low_half(0, 1))
            extra[1] += [lambda: w_low_half(1, 0), lambda: w_low_half(1, 1)]
            for w in range(2, NW):
                if w in DVE_MEASURES:
                    extra[W_AT[w] - 1].append(lambda w=w: w_measure(w))
                extra[W_AT[w]].append(lambda w=w: w_scales(w))
                extra[W_AT[w] + 1].append(lambda w=w: w_low(w))
            extra[4].append(labels_in)
            extra[8].append(count_fours)
            extra[11].append(count_pairs)
            extra[13].append(place_slots)
            extra[15].append(fill_slots)
            extra[17].append(name_slots)
            extra[7].append(lambda: x_measure(1, 1, TG, 16, x_inv_early[:, 1, :]))
            extra[10].append(lambda: x_low(1, 1, TG))
            extra[18].append(f_measure)
            extra[20].append(f_low)
            extra[25].append(lambda: x_measure(e_x(0), 0, EG, 16 + 16 * SLOTS, None))
            extra[27].append(lambda: x_low(e_x(0), 0, EG))
            steps(0, EARLY * SH, TOK, extra)
            beside = {2 * i + 2: (lambda i=i: load_expert(0, 0, quad(0), i),) for i in range(4)}
            beside[1] = (lambda: look_up(0, quad(0)),)
            beside[10] = (undo_scales,)
            beside[SH - 1] = (lambda: look_up(1, pair(0)),)
            steps(STEP_M, SH, B, beside)

            def job_measure(t, par, job):
                x_measure(e_x(t), par, job[2] * S // P, 16 + 16 * (slots_before(t, par) + job[2]), None)

            def weights_beside(t, par, job, at):
                return {q: [lambda i=i: load_expert(t, par, job, i)] for i, q in enumerate(at)}

            def four_job(t, n):
                ex = weights_beside(t + 1, 1, pair(n), (1, 2, 4, 5))
                ex[0] = [lambda: job_measure(t + 1, 1, pair(n))]
                ex[2].insert(0, lambda: x_low(e_x(t + 1), 1, PTOK // P))
                ex[3] = [lambda: job_measure(t + 2, 0, quad(n + 1))]
                ex[6] = [lambda: x_low(e_x(t + 2), 0, EG)]
                steps(e_step(t), FC, ETOK, ex)

            def pair_job(t, m):
                ex = weights_beside(t + 1, 0, quad(m + 1), (1, 2, 4, 5))
                ex[0] = [lambda: look_up(0, quad(m + 1))]
                ex[FC - 1] = [lambda: look_up(1, pair(m + 1) if not isinstance(m, int) else quad(QUADS - 1))]
                steps(e_step(t), FC, PTOK, ex)

            four_job(0, 0)
            with dve.Fori(0, PAIRS - 1) as i:
                t = 2 * i + 1
                pair_job(t, i)
                four_job(t + 1, i + 1)
            t = JOBS - 3
            pair_job(t, PAIRS - 1)
            ex = weights_beside(t + 2, 1, quad(QUADS - 1), (1, 3, 4, 5))
            ex[0] = [lambda: job_measure(t + 2, 1, quad(QUADS - 1))]
            ex[2] = [lambda: x_low(e_x(t + 2), 1, EG)]
            steps(e_step(t + 1), FC, ETOK, ex)
            n = b_x(EARLY)
            xp = n % 2
            loads_e = {0: 16 + 16 * SLOTS * (QUADS - 1), 1: 16 + 16 * (2 * PAIRS + SLOTS)}

            def tile_loads(u, par):
                first = EARLY if par == xp else EARLY + 1
                return loads_e[par] + 16 * ((u - first) // 2 + 1)

            steps(e_step(t + 2), FC, ETOK, {1: (lambda: x_measure(n, xp, TG, tile_loads(EARLY, xp), x_inv[:, xp, :]),),
                           3: (lambda: x_low(n, xp, TG),)})

            n_g = [0]

            def g_op(ins):
                n_g[0] += 1
                ins.then_inc(gate_dve, 1)
                dve.wait_ge(gate_dve, n_g[0])

            def gate_rows():
                dve.wait_ge(ef_loaded, 16)
                g_op(dve.tensor_scalar(gate_in[:, 0, :], e_first, f_fac[:, 0:1], None, ALU.mult))
                g_op(dve.tensor_copy(pw[:, 0, 0:1], lab_inv[:, NE:NE + 1]))

            def gate_turned():
                dve.wait_ge(gate_pe, 1)
                g_op(dve.tensor_copy(gate_T.rearrange("p j b -> p (j b)"), tr[0][:, 0:K3 * DC * B]))

            def gate_relu():
                dve.wait_ge(gate_pe, 2)
                g_op(dve.tensor_scalar(gate_h.rearrange("p m b -> p (m b)"), tr[1][:, 0:DC * B], 0.0, None, ALU.max))

            def gate_max():
                dve.wait_ge(gate_pe, 3)
                g_op(dve.tensor_copy(logit[:, :], tr[0][0:B, 0:K3]))
                g_op(dve.tensor_reduce(lmax[:, :], logit[:, :], AX.X, ALU.max, negate=True))

            def gate_soft():
                dve.wait_ge(const_done, 8)
                dve.wait_ge(gate_act, 1)
                g_op(dve.tensor_reduce(psum_[:, :], prob[:, :], AX.X, ALU.add))
                g_op(dve.reciprocal(prec[:, :], psum_[:, :]))
                g_op(dve.tensor_copy(pw[:, 0, 1:K3], pair_inv[0:B, 0:NSH]))
                g_op(dve.scalar_tensor_tensor(out=pw[:, 1, :], in0=prob[:, :], scalar=prec[:, 0:1], in1=pw[:, 0, :],
                                              op0=ALU.mult, op1=ALU.mult))
                g_op(dve.tensor_tensor(spread[:, :, :],
                                       group[:, :].rearrange("b (g o) -> b g o", o=1).to_broadcast([B, GROUPS, K3]),
                                       pw[:, 1:2, :].to_broadcast([B, GROUPS, K3]), ALU.mult))

            def gate_out():
                dve.wait_ge(gate_pe, 4)
                g_op(dve.tensor_copy(w_tok[:, :, :].rearrange("p g k -> p (g k)"), tr[1][:, 0:GROUPS * K3]))

            def base(u, par, inv, n_en):
                dve.wait_ge(x_inv_done, u + 1)
                dve.tensor_tensor(fac[:, par], one_tile(u), inv, ALU.mult).then_inc(fac_done, 1)
                dve.wait_ge(fac_done, u - EARLY + 1)
                dve.wait_ge(en_loaded[par], n_en)
                xb = b_x(par) % 2
                for g in range(TG):
                    i = dve.scalar_tensor_tensor(out=acc[par][:, g, :], in0=e_nat[par][:, g, :], scalar=fac[:, par, g, 0:1],
                                                 in1=x_nat[:, xb, g, :], op0=ALU.mult, op1=ALU.add)
                i.then_inc(base_done, 1)

            def one_tile(u):
                return w_tok[:, TG * u:TG * (u + 1), :] if isinstance(u, int) else w_tok[:, bass.ds(TG * u, TG), :]

            def combine(u, par, k):
                dve.wait_ge(h_used, b_step(u) + (k + 1) * FC)
                if k == 0:
                    dve.wait_ge(base_done, u - EARLY + 1)
                else:
                    dve.wait_ge(combined, b_combined(u, 0))
                for g in range(TG):
                    i = dve.scalar_tensor_tensor(out=acc[par][:, g, :], in0=accb[2 * k + g // 2][:, (g % 2) * D:(g % 2 + 1) * D],
                                                 scalar=fac[:, par, g, 1 + k:2 + k], in1=acc[par][:, g, :],
                                                 op0=ALU.mult, op1=ALU.add)
                i.then_inc(combined, 1)

            def inv_of(par):
                xb = b_x(par) % 2
                return x_inv[:, xb, :].rearrange("p (g o) -> p g o", o=1).to_broadcast([P, TG, K3])

            def early_factors():
                dve.wait_ge(early_loaded, 32 * EARLY)
                for i in range(EARLY):
                    dve.tensor_tensor(fac_early[:, i], w_tok[:, TG * i:TG * (i + 1), :],
                                      x_inv_early[:, i, :].rearrange("p (g o) -> p g o", o=1).to_broadcast([P, TG, K3]),
                                      ALU.mult).then_inc(early_step, 1)
                dve.wait_ge(early_step, EARLY)

            def early_term(i, k):
                rows = e_early[i] if k == 0 else s_early[:, i, k - 1]
                for g in range(TG):
                    a = dve.scalar_tensor_tensor(out=x_early[i][:, g, :], in0=rows[:, g, :],
                                                 scalar=fac_early[:, i, g, k:k + 1],
                                                 in1=x_early[i][:, g, :], op0=ALU.mult, op1=ALU.add)
                a.then_inc(early_step, 1)
                dve.wait_ge(early_step, EARLY + K3 * i + k + 1)

            def tile(u, par, extra, n_next=None):
                m = {q: tuple(v) for q, v in extra.items()}
                if n_next is not None:
                    xb = b_x(par + 1) % 2
                    m[5] = m.get(5, ()) + (lambda: x_measure(b_x(u + 1), xb, TG, n_next, x_inv[:, xb, :]),)
                    m[7] = m.get(7, ()) + (lambda: x_low(b_x(u + 1), xb, TG),)
                steps(b_step(u), SH, TOK, m)

            def en_count(u, par):
                return 16 * ((u - par) // 2)

            def usual(u, par):
                return {2: (lambda: combine(u - 1, 1 - par, 1),), 3: (lambda: base(u, par, inv_of(par), en_count(u, par)),),
                        11: (lambda: combine(u, par, 0),)}

            tile(EARLY, 0, {6: (gate_rows,), 7: (gate_turned,), 8: (gate_relu,), 9: (gate_max,), 10: (gate_soft,),
                            12: (gate_out,),
                            13: (lambda: base(EARLY, 0, inv_of(0), 16),), 14: (lambda: combine(EARLY, 0, 0),)},
                 tile_loads(EARLY + 1, 1 - xp))
            with dve.Fori(0, (TILES - EARLY - 2) // 2) as i:
                u = 2 * i + EARLY + 1
                tile(u, 1, usual(u, 1), tile_loads(u + 1, xp))
                tile(u + 1, 0, usual(u + 1, 0), tile_loads(u + 2, 1 - xp))
            last = usual(TILES - 1, 1)
            last[4] = (early_factors,)
            for i in range(EARLY):
                for k in range(K3):
                    last.setdefault(5 + K3 * i + k, ())
                    last[5 + K3 * i + k] += (lambda i=i, k=k: early_term(i, k),)
            tile(TILES - 1, 1, last)
            combine(TILES - 1, 1, 1)


F_FAC = 12
N_COUNTED, N_PLACED = 8, 32

W_AT = {2: 2, 3: 5, 4: 8, 5: 11, 6: 13, 7: 15, 8: 18, 9: 20, 10: 23, 11: 25, 12: 28, 13: 30}
DVE_MEASURES = (0, 1, 10, 12)


def measured(w):
    return sum((v in DVE_MEASURES) == (w in DVE_MEASURES) for v in range(w + 1))


_INS = ['x', 'itok_B_0_2', 'L0_cond_wi', 'L0_cond_wo', 'L0_cond_swi', 'L0_cond_swo', 'L0_cond_g1', 'L0_cond_g2']


def kernel(**inputs):
    import numpy as _np
    import concourse.bacc as _bacc
    from concourse import mybir as _mybir
    from concourse.bass_utils import run_bass_kernel_spmd as _run

    nc = _bacc.Bacc("TRN2", target_bir_lowering=False, num_devices=1)
    arrays, args = {}, []
    for name in _INS:
        a = _np.ascontiguousarray(inputs[name])
        arrays[f"in_{name}_dram"] = a
        args.append(nc.dram_tensor(f"in_{name}_dram", a.shape, _mybir.dt.from_np(a.dtype), kind="ExternalInput").ap())
    shape = inputs['x'].shape
    args.append(nc.dram_tensor("out_0_dram", shape, _mybir.dt.float32, kind="ExternalOutput").ap())
    build(nc, *args)
    r = _run(nc, [arrays], core_ids=[0])
    return r.results[0]["out_0_dram"]
```
